# Optimizing a Trainium2 kernel written in Bass

```python
import numpy as np
import jax
import jax.numpy as jnp

def _softmax(x, axis=-1):
    return jax.nn.softmax(x, axis=axis)

def _gelu(x):
    return jax.nn.gelu(x, approximate=True)

def _silu(x):
    return jax.nn.silu(x)

def _sigmoid(x):
    return jax.nn.sigmoid(x)

def _layernorm(x, axis=-1, eps=1e-05):
    m = jnp.mean(x, axis=axis, keepdims=True)
    v = jnp.var(x, axis=axis, keepdims=True)
    return (x - m) / jnp.sqrt(v + eps)

def _scatter_add(tgt, idx, src, axis=0):
    return tgt.at[idx].add(src)

def _segment_sum(src, seg, n):
    return jax.ops.segment_sum(src, seg, n)
kernel_name = 'mk_adaln_d1_jaxref_r4_f38356'

def setup_inputs(seed: int=0):
    np.random.seed(seed)
    _w = jnp.asarray

    def _L0_attn_setup():
        import jax, jax.numpy as jnp
        import numpy as np
        HEADS = 16
        DIM_HEAD = 64
        SCALE = DIM_HEAD ** (-0.5)
        key = jax.random.key(seed)
        k1, k2, k3 = jax.random.split(key, 3)
        B, N, D = (4, 1024, 256)
        inner = HEADS * DIM_HEAD
        x = jax.random.normal(k1, (B, N, D), dtype=jnp.float32)
        w_qkv = jax.random.normal(k2, (D, 3 * inner), dtype=jnp.float32) * D ** (-0.5)
        w_out = jax.random.normal(k3, (inner, D), dtype=jnp.float32) * inner ** (-0.5)
        b_out = jnp.zeros((D,), dtype=jnp.float32)
        return {'x': x, 'w_qkv': w_qkv, 'w_out': w_out, 'b_out': b_out}
    _L0_attn_in = _L0_attn_setup()

    def _L0_ffn_setup():
        import jax, jax.numpy as jnp
        import numpy as np
        B, S, F, E, K = (4, 256, 256, 8, 2)
        H = 4 * F
        key = jax.random.key(seed)
        ks = jax.random.split(key, 7)

        def xavier(k, shape):
            fan_in, fan_out = (shape[-2], shape[-1])
            scale = jnp.sqrt(6.0 / (fan_in + fan_out))
            return jax.random.uniform(k, shape, jnp.float32, -scale, scale)
        return {'x': jax.random.normal(ks[0], (B, S, F), jnp.float32), 'Wg': xavier(ks[1], (F, E)), 'bg': jnp.zeros((E,), jnp.float32), 'W1': xavier(ks[2], (E, F, H)), 'b1': jnp.zeros((E, H), jnp.float32), 'W2': xavier(ks[3], (E, H, F)), 'b2': jnp.zeros((E, F), jnp.float32)}
    _L0_ffn_in = _L0_ffn_setup()
    _L0_c = _w((lambda *s: np.random.randn(*s).astype(np.float32) * 0.05)(1, 256))
    _L0_wmod = _w((lambda *s: np.random.randn(*s).astype(np.float32) * 0.05)(256, 6 * 256) * 256 ** (-0.5))
    _d = {'L0_attn_x': _L0_attn_in['x'], 'L0_attn_w_qkv': _L0_attn_in['w_qkv'], 'L0_attn_w_out': _L0_attn_in['w_out'], 'L0_attn_b_out': _L0_attn_in['b_out'], 'L0_ffn_Wg': _L0_ffn_in['Wg'], 'L0_ffn_bg': _L0_ffn_in['bg'], 'L0_ffn_W1': _L0_ffn_in['W1'], 'L0_ffn_b1': _L0_ffn_in['b1'], 'L0_ffn_W2': _L0_ffn_in['W2'], 'L0_ffn_b2': _L0_ffn_in['b2'], 'L0_c': _L0_c, 'L0_wmod': _L0_wmod}
    _x0 = _d['L0_attn_x']
    _d['L0_attn_x'] = jax.random.normal(jax.random.fold_in(jax.random.key(seed), 1), (1, 4096, 256), dtype=_x0.dtype)
    del _x0
    return _d

def reference(L0_attn_x, L0_attn_w_qkv, L0_attn_w_out, L0_attn_b_out, L0_ffn_Wg, L0_ffn_bg, L0_ffn_W1, L0_ffn_b1, L0_ffn_W2, L0_ffn_b2, L0_c, L0_wmod):

    def _L0_attn_ref(x, w_qkv, w_out, b_out):
        import jax, jax.numpy as jnp
        import numpy as np
        HEADS = 16
        DIM_HEAD = 64
        SCALE = DIM_HEAD ** (-0.5)
        B, N, D = x.shape
        inner = HEADS * DIM_HEAD
        qkv = x @ w_qkv
        q, k, v = jnp.split(qkv, 3, axis=-1)

        def to_heads(t):
            return t.reshape(B, N, HEADS, DIM_HEAD).transpose(0, 2, 1, 3)
        q, k, v = (to_heads(q), to_heads(k), to_heads(v))
        q = jax.nn.softmax(q * SCALE, axis=-1)
        k = jax.nn.softmax(k, axis=-2)
        context = jnp.einsum('bhnd,bhne->bhde', q, k)
        out = jnp.einsum('bhde,bhnd->bhne', context, v)
        out = out.transpose(0, 2, 1, 3).reshape(B, N, inner)
        return out @ w_out + b_out

    def _L0_ffn_ref(x, Wg, bg, W1, b1, W2, b2):
        import jax, jax.numpy as jnp
        import numpy as np
        B, S, F, E, K = (4, 256, 256, 8, 2)
        H = 4 * F
        gate_probs = jax.nn.softmax(x @ Wg + bg, axis=-1)
        k = K
        _, top_idx = jax.lax.top_k(gate_probs, k)
        expert_mask = jax.nn.one_hot(top_idx, gate_probs.shape[-1], dtype=gate_probs.dtype).sum(-2)
        selected = gate_probs * expert_mask
        selected = selected / (selected.sum(-1, keepdims=True) + 1e-08)
        h = jax.nn.gelu(jnp.einsum('bsf,efh->bseh', x, W1) + b1)
        expert_out = jnp.einsum('bseh,ehf->bsef', h, W2) + b2[None, None]
        return jnp.einsum('bsef,bse->bsf', expert_out, selected)
    x = L0_attn_x
    mod = (_silu(L0_c) @ L0_wmod).reshape(L0_c.shape[0], 6, 1, -1)
    sa, ca, ga, sb, cb, gb = (mod[:, 0], mod[:, 1], mod[:, 2], mod[:, 3], mod[:, 4], mod[:, 5])
    ga = (2 * (ga >= 0) - 1) * jnp.maximum(jnp.abs(ga), 0.25)
    gb = (2 * (gb >= 0) - 1) * jnp.maximum(jnp.abs(gb), 0.25)
    h = _layernorm(x, axis=-1) * (1 + ca) + sa
    x = x + ga * _L0_attn_ref(h, L0_attn_w_qkv, L0_attn_w_out, L0_attn_b_out)
    h = _layernorm(x, axis=-1) * (1 + cb) + sb
    x = x + gb * _L0_ffn_ref(h, L0_ffn_Wg, L0_ffn_bg, L0_ffn_W1, L0_ffn_b1, L0_ffn_W2, L0_ffn_b2)
    return x

_drawn_inputs = setup_inputs


def setup_inputs(seed=0):
    import zlib

    import numpy as np

    out = dict(_drawn_inputs(seed))
    spreads = {'L0_attn_b_out': (0.0, 0.32),
     'L0_ffn_bg': (0.0, 0.504),
     'L0_ffn_b1': (0.0, 0.512),
     'L0_ffn_b2': (0.0, 0.417)}
    factors = {}
    for name, (base, spread) in spreads.items():
        noise = np.random.default_rng([zlib.crc32(name.encode()), seed]).standard_normal(out[name].shape)
        drawn = base * np.exp(spread * noise) if base else spread * noise
        out[name] = jnp.asarray(drawn.astype(out[name].dtype))
    for name, factor in factors.items():
        out[name] = (out[name] * factor).astype(out[name].dtype)
    return out
```

```python
from contextlib import ExitStack

import concourse.bass as bass
from concourse import mybir

F32 = mybir.dt.float32
F32R = mybir.dt.float32r
BF16 = mybir.dt.bfloat16
I32 = mybir.dt.int32
ALU = mybir.AluOpType
ACT = mybir.ActivationFunctionType
AX = mybir.AxisListType.X

P = 128
N = 4096
D = 256
C = D // P
HD = 1024
J = HD // P
DH = 64
TILES = N // P
ST = 4
SBN = TILES // ST
STOK = ST * P
E = 8
FH = 1024
M = FH // P
GT = 8
GROUPS = TILES // GT
BT = 256
BI = BT // P
CAP = N + BT
ROW = D + E + 1
MAXB = N // BT
EPS = 1e-5
SCALE = DH ** -0.5
BIG = 3.0e38


def bc(ap, axis, shape):
    return ap.unsqueeze(axis).to_broadcast(shape)


class Link:

    def __init__(self, eng, sem):
        self.eng, self.sem, self.base, self.n = eng, sem, 0, 0

    def link(self, ins):
        self.n += 1
        ins.then_inc(self.sem, 1)
        self.eng.wait_ge(self.sem, self.base + self.n)

    def link_apart(self, ins, turn):
        self.link(ins)
        self.eng.sem_inc(turn, 1)

    def enter(self, reg):
        self.reg = reg
        self.eng.reg_mov(reg, self.base + self.n)
        self.begin()

    def begin(self):
        self.n = 0
        self.base = self.eng.snap(self.reg, min_val=0, max_val=60000)

    def end(self):
        self.eng.reg_add(self.reg, self.reg, self.n)
        self.n = 0


def adaln_block(nc, x, w_qkv, w_out, b_out, Wg, bg, W1, b1, W2, b2, cvec, wmod, out):
    ctx = ExitStack()
    with ctx:
        def sb(name, shape, dt, stack=ctx):
            return stack.enter_context(nc.sbuf_tensor(name, shape, dt))

        def sem(name):
            return ctx.enter_context(nc.semaphore(name))

        ps = ctx.enter_context(nc.psum_tensor("ps", [P, 8, 512], F32))

        ident = sb("ident", [P, P], F32)
        before_bf = sb("before_bf", [P, P], BF16)
        ones_bf = sb("ones_bf", [P, P], BF16)
        lane = sb("lane", [P, E], F32)
        list_start = sb("list_start", [P, E], F32)
        list_next = sb("list_next", [P, E], F32)
        token_of = sb("token_of", [P, GT], F32)
        ones_row = sb("ones_row", [1, P], F32)
        silu_c = sb("silu_c", [P, C], F32)
        silu_t = sb("silu_t", [P, C], F32)
        silu_b = sb("silu_b", [P, C, P], F32)
        modc = sb("modc", [P, 4, C], F32)
        shift_b = sb("shift_b", [P, C, P], F32)
        gates = sb("gates", [P, 2, D], F32)
        gate_s = sb("gate_s", [P, 2, D], F32)
        gate_m = sb("gate_m", [P, 2, D], F32)
        bo_bc = sb("bo_bc", [P, D], F32)
        wg_raw = sb("wg_raw", [P, C, E], F32)
        wg_mod = sb("wg_mod", [P, C, E], F32)
        bg_bc = sb("bg_bc", [P, E], F32)
        b1_rows = sb("b1_rows", [E * M, P], F32)
        b1_col = sb("b1_col", [P, E, M], F32)
        c_rows = sb("c_rows", [C, P], F32)
        counts_f = sb("counts_f", [P, E], F32)
        counts = sb("counts", [P, E], I32)
        blocks = sb("blocks", [P, E], I32)
        pad_id = sb("pad_id", [P, BI], I32)
        y_w = sb("y_w", [P, BI, E], F32)
        y_id = sb("y_id", [P, BI], I32)
        ctx_acc = sb("ctx_acc", [P, J, P], F32)
        k_sum = sb("k_sum", [P, J], F32)
        k_rec = sb("k_rec", [P, J], F32)
        wv_raw = sb("wv_raw", [P, C, HD], F32)
        wvT = sb("wvT", [P, J, D], F32)
        wout_sb = sb("wout_sb", [P, J, D], F32)

        a_stack = ExitStack()
        wqk_hi = sb("wqk_hi", [P, C, 2 * HD], F32R, a_stack)
        wqk_lo = sb("wqk_lo", [P, C, 2 * HD], F32R, a_stack)
        x_in = sb("x_in", [P, ST, D], F32, a_stack)
        xn = sb("xn", [P, ST, D], F32, a_stack)
        ln_s = sb("ln_s", [P, ST, 6], F32, a_stack)
        ln_a = sb("ln_a", [P, ST, 2], F32, a_stack)
        ln_v = sb("ln_v", [P, ST], F32, a_stack)
        ln_i = sb("ln_i", [P, ST], I32, a_stack)
        ln_t = sb("ln_t", [P, ST], F32, a_stack)
        ln_r = sb("ln_r", [P, ST], F32, a_stack)
        h_full = sb("h_full", [P, C, STOK], F32, a_stack)
        h_q = sb("h_q", [P, 2, C, STOK], F32R, a_stack)
        h_k = sb("h_k", [P, 2, 2, C, STOK], F32R, a_stack)
        k_exp = sb("k_exp", [P, 2, STOK], F32, a_stack)
        k_hi = sb("k_hi", [P, 2, ST, P], F32R, a_stack)
        k_lo = sb("k_lo", [P, 2, ST, P], F32R, a_stack)
        q_exp = sb("q_exp", [P, 2, HD], F32, a_stack)
        q_max = sb("q_max", [P, 2, 2 * J], F32, a_stack)
        q_sum = sb("q_sum", [P, 2, 2 * J], F32, a_stack)
        q_rec = sb("q_rec", [P, 2, 2 * J], F32, a_stack)
        ctx_t = sb("ctx_t", [P, P], F32, a_stack)
        k_blk = sb("k_blk", [P, J], F32, a_stack)
        k_nmax = sb("k_nmax", [P, J], F32, a_stack)
        k_dm = sb("k_dm", [P, J], F32, a_stack)
        k_alpha = sb("k_alpha", [P, J], F32, a_stack)
        k_part = sb("k_part", [P, J], F32, a_stack)
        setup_stack = ExitStack()
        wqk_raw = sb("wqk_raw", [P, C, 2 * HD], F32, setup_stack)
        wmod_sb = sb("wmod_sb", [P, C, 6 * D], F32, setup_stack)
        setup_stack.close()
        q_hl = sb("q_hl", [P, 2, ST, J, 2, P], F32R, a_stack)
        a_stack.close()

        b_stack = ExitStack()
        w1_hi = [sb("w1_hi0", [P, C, FH], F32R, b_stack)]
        w1_lo = [sb("w1_lo0", [P, C, FH], F32R, b_stack)]
        w2_hi = [sb("w2_hi0", [P, M, D], F32R, b_stack)]
        w2_lo = [sb("w2_lo0", [P, M, D], F32R, b_stack)]
        w1_raw = sb("w1_raw", [P, C, FH], F32, b_stack)
        w2_raw = sb("w2_raw", [P, M, D], F32, b_stack)
        b2_bc = sb("b2_bc", [P, E, D], F32, b_stack)
        listed = sb("listed", [P, BI, ROW], F32, b_stack)
        pad = sb("pad", [P, BI, ROW], F32, b_stack)
        bb_stack = ExitStack()
        ctx_n = sb("ctx_n", [P, J, P], F32, bb_stack)
        cw = sb("cw", [P, J, D], F32, bb_stack)
        fold = sb("fold", [P, C, D], F32, bb_stack)
        fold_hi = sb("fold_hi", [P, C, D], F32R, bb_stack)
        fold_lo = sb("fold_lo", [P, C, D], F32R, bb_stack)
        h_b = sb("h_b", [P, 2, 2, 2, C, STOK], F32R, bb_stack)
        x_b = sb("x_b", [P, 2, GT, D], F32, bb_stack)
        x1 = sb("x1", [P, GT, D], F32, bb_stack)
        bn_s = sb("bn_s", [P, GT, 6], F32, bb_stack)
        bn_a = sb("bn_a", [P, GT, 2], F32, bb_stack)
        bn_v = sb("bn_v", [P, GT], F32, bb_stack)
        bn_i = sb("bn_i", [P, GT], I32, bb_stack)
        bn_t = sb("bn_t", [P, GT], F32, bb_stack)
        bn_r = sb("bn_r", [P, GT], F32, bb_stack)
        x1T = sb("x1T", [P, 2, D], F32, bb_stack)
        rows = sb("rows", [P, 2, GT, ROW], F32, bb_stack)
        probs = sb("probs", [P, GT, E], F32, bb_stack)
        cand = sb("cand", [P, GT, E], F32, bb_stack)
        rest = sb("rest", [P, GT, E], F32, bb_stack)
        pick = sb("pick", [P, 2, GT, E], F32, bb_stack)
        chosen = sb("chosen", [P, GT, E], F32, bb_stack)
        chosen_bf = sb("chosen_bf", [P, GT + 1, E], BF16, bb_stack)
        red = sb("red", [P, GT], F32, bb_stack)
        spot = sb("spot", [P, GT, E], F32, bb_stack)
        spot_k = sb("spot_k", [P, 2, GT], F32, bb_stack)
        spot_i = sb("spot_i", [P, 2, GT, 2], I32, bb_stack)
        bb_stack.close()
        c_stack = ExitStack()
        w1_hi.append(sb("w1_hi1", [P, C, FH], F32R, c_stack))
        w1_lo.append(sb("w1_lo1", [P, C, FH], F32R, c_stack))
        w2_hi.append(sb("w2_hi1", [P, M, D], F32R, c_stack))
        w2_lo.append(sb("w2_lo1", [P, M, D], F32R, c_stack))
        xT_full = sb("xT_full", [P, C, BT], F32, c_stack)
        xT_hi = sb("xT_hi", [P, C, BT], F32R, c_stack)
        xT_lo = sb("xT_lo", [P, C, BT], F32R, c_stack)
        hid = sb("hid", [P, M, BT], F32, c_stack)
        hid_hi = sb("hid_hi", [P, M, BT], F32R, c_stack)
        hid_lo = sb("hid_lo", [P, M, BT], F32R, c_stack)
        y = sb("y", [P, BI, D], F32, c_stack)
        c_stack.close()
        b_stack.close()

        lists = nc.dram_tensor("lists", [E * CAP, ROW], F32).ap()
        h_store = nc.dram_tensor("h_store", [SBN, 2, P, C, STOK], F32).ap()

        s_c = sem("s_c")
        s_wmod = sem("s_wmod")
        s_wqk = sem("s_wqk")
        s_small = sem("s_small")
        s_fold_in = sem("s_fold_in")
        s_const = sem("s_const")
        s_cT = sem("s_cT")
        s_cTc = sem("s_cTc")
        s_silu_e = sem("s_silu_e")
        s_silu = sem("s_silu")
        s_mod = sem("s_mod")
        s_modr = sem("s_modr")
        s_bgp = sem("s_bgp")
        s_bgr = sem("s_bgr")
        s_whqk = sem("s_whqk")
        s_wlqk = sem("s_wlqk")
        s_wvT = sem("s_wvT")
        s_wvTc = sem("s_wvTc")
        s_x = sem("s_x")
        s_xn = sem("s_xn")
        s_xt = sem("s_xt")
        s_hhi = sem("s_hhi")
        s_hlo = sem("s_hlo")
        s_hk = sem("s_hk")
        s_hst = sem("s_hst")
        s_kt = sem("s_kt")
        s_nm = sem("s_nm")
        s_ke = sem("s_ke")
        s_al = sem("s_al")
        s_kT = sem("s_kT")
        s_khi = sem("s_khi")
        s_klo = sem("s_klo")
        s_ctx = sem("s_ctx")
        s_acc = sem("s_acc")
        s_q = sem("s_q")
        s_qs = sem("s_qs")
        s_qe = sem("s_qe")
        s_qr = sem("s_qr")
        s_qn = sem("s_qn")
        s_qhi = sem("s_qhi")
        s_qlo = sem("s_qlo")
        s_ctxn = sem("s_ctxn")
        s_cw = sem("s_cw")
        s_cwc = sem("s_cwc")
        s_fold = sem("s_fold")
        s_foldr = sem("s_foldr")
        s_xb = [sem(f"s_xb{i}") for i in range(2)]
        s_hb = [sem(f"s_hb{i}") for i in range(2)]
        s_at = sem("s_at")
        s_x1 = sem("s_x1")
        s_x1out = [sem(f"s_x1out{i}") for i in range(2)]
        s_row = sem("s_row")
        s_rT = sem("s_rT")
        s_rTc = sem("s_rTc")
        s_lg = sem("s_lg")
        s_lgs = sem("s_lgs")
        s_pe = sem("s_pe")
        s_ch = sem("s_ch")
        s_rk = sem("s_rk")
        s_spot = sem("s_spot")
        s_list = [sem(f"s_list{i}") for i in range(2)]
        s_free = [sem(f"s_free{i}") for i in range(2)]
        s_counts = sem("s_counts")
        s_pad = sem("s_pad")
        s_padw = sem("s_padw")
        s_b2 = sem("s_b2")
        s_wraw = sem("s_wraw")
        s_whi = sem("s_whi")
        s_wlo = sem("s_wlo")
        s_rows = sem("s_rows")
        s_meta = sem("s_meta")
        s_bt = sem("s_bt")
        s_bhi = sem("s_bhi")
        s_blo = sem("s_blo")
        s_f1 = sem("s_f1")
        s_gelu = sem("s_gelu")
        s_hid = sem("s_hid")
        s_f2 = sem("s_f2")
        s_y = sem("s_y")
        s_added = sem("s_added")
        s_done = sem("s_done")
        s_turn = sem("s_turn")
        s_turn_dve = sem("s_turn_dve")
        s_turn_pe = sem("s_turn_pe")
        s_turn_pool = sem("s_turn_pool")
        s_dve = sem("s_dve")
        s_pool = sem("s_pool")

        TWO = 2
        FOUR = 4
        ONE = 1
        DMA2 = 32
        LISTED = 16 * 2 * GT
        G_END = 2 * LISTED
        CREDIT = 16

        KT, TR, CX = 4, 6, 7
        AT, RT, LG, RK = 0, 2, 4, 6
        XTB, Y0 = 4, 5

        x_t = x.rearrange("a (t p) d -> p (a t) d", p=P)
        out_t = out[0:N, :].rearrange("(t p) d -> p t d", p=P)

        def three(pairs):
            ops = [(a, b) for (ah, al), (bh, bl) in pairs for a, b in ((ah, bh), (ah, bl), (al, bh))]
            return [(a, b, i == 0, i == len(ops) - 1) for i, (a, b) in enumerate(ops)]

        def superblocks(eng, body):
            with eng.Fori(0, SBN - 2) as s:
                body(s, True, True)
            body(SBN - 2, True, False)
            body(SBN - 1, False, False)

        def experts(eng, reg, body):
            def one(e, par, last):
                nb = eng.value_load(blocks[0:1, bass.ds(e, 1)], min_val=1, max_val=MAXB)
                body(e, par, nb, last)
            with eng.Fori(0, E // 2 - 1) as ep:
                one(ep * 2, 0, False)
                one(ep * 2 + 1, 1, False)
            one(E - 2, 0, False)
            one(E - 1, 1, True)

        def block_counter(eng, name):
            reg = eng.alloc_register(name)
            eng.reg_mov(reg, 0)
            return reg

        def now(eng, reg):
            return eng.snap(reg, min_val=0, max_val=N // BT * 2 + E)

        block = ctx.enter_context(nc.Block())

        @block.sync
        def _(sp):
            def wait_reg(s, value):
                sp.wait_ge(s, value)
                sp.sem_inc(s_turn, 1)

            for s in s_x1out:
                sp.sem_inc(s, CREDIT)
            sp.dma_start(c_rows[:, :], cvec.rearrange("a (c p) -> (a c) p", p=P)).then_inc(s_c, 16)
            sp.dma_start(b1_rows[:, :], b1.rearrange("e (m p) -> (e m) p", p=P)).then_inc(s_c, 16)
            sp.dma_start(x_in[:, :, :], x_t[:, 0:ST, :]).then_inc(s_x, 16)
            sp.dma_start(wmod_sb[:, :, :], wmod.rearrange("(c p) n -> p c n", p=P)).then_inc(s_wmod, 16)
            sp.dma_start(wqk_raw[:, :, :], w_qkv[:, 0:2 * HD].rearrange("(c p) n -> p c n", p=P)).then_inc(s_wqk, 16)
            sp.dma_start(bo_bc[:, :], b_out.partition_broadcast(P)).then_inc(s_small, 16)
            sp.dma_start(bg_bc[:, :], bg.partition_broadcast(P)).then_inc(s_small, 16)
            sp.dma_start(wg_raw[:, :, :], Wg.rearrange("(c p) e -> p c e", p=P)).then_inc(s_small, 16)
            sp.dma_start(wv_raw[:, :, :], w_qkv[:, 2 * HD:3 * HD].rearrange("(c p) n -> p c n", p=P)).then_inc(s_fold_in, 16)
            sp.dma_start(wout_sb[:, :, :], w_out.rearrange("(j p) n -> p j n", p=P)).then_inc(s_fold_in, 16)

            def spread(s, load_next, reuse):
                if load_next:
                    wait_reg(s_xn, s + 1)
                    sp.dma_start(x_in[:, :, :], x_t[:, bass.ds((s + 1) * ST, ST), :]).then_inc(s_x, 16)
                if reuse:
                    wait_reg(s_kt, (s - 1) * J)
                wait_reg(s_hlo, (s + 1) * C)
                par = s & 1
                sp.dma_start(h_k[:, bass.ds(par, 1), :, :, :].rearrange("p a b c t -> p (a b c t)").bitcast(F32),
                             h_q[:, :, :, :].rearrange("p b c t -> p (b c t)").bitcast(F32)).then_inc(s_hk, 16)
                sp.dma_start(h_store[bass.ds(s, 1), :, :, :, :].rearrange("a b p c t -> p (a b) (c t)"),
                             h_q[:, :, :, :].rearrange("p b c t -> p b (c t)").bitcast(F32)).then_inc(s_hst, 16)

            spread(0, True, False)
            spread(1, True, False)
            with sp.Fori(2, SBN - 1) as s:
                spread(s, True, True)
            spread(SBN - 1, False, True)

            sp.wait_ge(s_ctx, SBN * J + TWO)
            sp.wait_ge(s_acc, SBN * J + TWO)
            sp.wait_ge(s_qlo, TILES)
            sp.wait_ge(s_al, SBN * J)
            sp.wait_ge(s_hk, 16 * SBN)
            sp.wait_ge(s_hst, 16 * SBN)

            def load_group(g):
                par = g % 2
                if g >= 2:
                    sp.wait_ge(s_row, (g - 1) * GT)
                    sp.wait_ge(s_at, (g - 1) * GT)
                for part in range(2):
                    for u in range(2):
                        sp.dma_start(h_b[:, par, part, u, :, :].rearrange("p c t -> p (c t)").bitcast(F32),
                                     h_store[2 * g + u, part, :, :, :].rearrange("p c t -> p (c t)")).then_inc(s_hb[par], 16)
                sp.dma_start(x_b[:, par, :, :], x_t[:, g * GT:(g + 1) * GT, :]).then_inc(s_xb[par], 16)

            load_group(0)
            sp.dma_start(w1_raw[:, :, :], W1[0, :, :].rearrange("(c p) n -> p c n", p=P)).then_inc(s_wraw, 16)
            sp.dma_start(w2_raw[:, :, :], W2[0, :, :].rearrange("(m p) n -> p m n", p=P)).then_inc(s_wraw, 16)
            sp.dma_start(b2_bc[:, :, :].rearrange("p e d -> p (e d)"), b2.rearrange("e d -> (e d)").partition_broadcast(P)).then_inc(s_b2, 16)
            load_group(1)
            sp.wait_ge(s_pad, 2)
            for g in range(GROUPS):
                if 1 <= g < GROUPS - 1:
                    load_group(g + 1)
                for half in range(2):
                    sp.wait_ge(s_x1, g * GT + half * 4 + 4 + FOUR)
                    t0 = g * GT + half * 4
                    sp.dma_start(out_t[:, t0:t0 + 4, :], x1[:, half * 4:half * 4 + 4, :]).then_inc(s_x1out[half], 16)
            sp.wait_ge(s_counts, 1)
            with sp.Fori(0, E) as e:
                n = sp.value_load(counts[0:1, bass.ds(e, 1)], min_val=0, max_val=N)
                sp.dma_start(lists[bass.ds(e * CAP + n, BT), :].rearrange("(p i) c -> p i c", i=BI), pad[:, :, :]).then_inc(s_padw, 16)
            sp.wait_ge(s_padw, 16 * E)
            for par in range(2):
                sp.wait_ge(s_list[par], G_END)

            g = block_counter(sp, "g_sp")

            def load_rows(e, b):
                gv = now(sp, g)
                wait_reg(s_meta, gv + ONE)
                wait_reg(s_bt, gv + ONE)
                sp.dma_start(listed[:, :, :], lists[bass.ds(e * CAP + b * BT, BT), :].rearrange("(p i) c -> p i c", i=BI)).then_inc(s_rows, 16)
                sp.reg_add(g, g, 1)

            def expert(e, par, nb, last):
                if not last:
                    wait_reg(s_wlo, e + 1)
                    sp.dma_start(w1_raw[:, :, :], W1[bass.ds(e + 1, 1), :, :].rearrange("a (c p) n -> p (a c) n", p=P)).then_inc(s_wraw, 16)
                    sp.dma_start(w2_raw[:, :, :], W2[bass.ds(e + 1, 1), :, :].rearrange("a (m p) n -> p (a m) n", p=P)).then_inc(s_wraw, 16)
                with sp.Fori(0, nb) as b:
                    load_rows(e, b)

            experts(sp, g, expert)
            load_rows(0, 0)
            sp.wait_ge(s_done, 1)
            for half in range(2):
                sp.wait_ge(s_x1out[half], 16 * GROUPS + CREDIT)

        @block.gpsimd
        def _(pool):
            for s in s_free:
                pool.sem_inc(s, 1)
            pool.memset(ident[:, :], 0.0).then_inc(s_pool, 1)
            pool.memset(before_bf[:, :], 1.0).then_inc(s_pool, 1)
            pool.wait_ge(s_pool, 2)
            pool.affine_select(out=ident[:, :], in_=ident[:, :], compare_op=ALU.not_equal, fill=1.0,
                               base=0, pattern=[[-1, P]], channel_multiplier=1).then_inc(s_const, 1)
            pool.affine_select(out=before_bf[:, :], in_=before_bf[:, :], compare_op=ALU.is_gt, fill=0.0,
                               base=0, pattern=[[1, P]], channel_multiplier=-1).then_inc(s_const, 1)
            pool.memset(ones_bf[:, :], 1.0).then_inc(s_const, 1)
            pool.memset(ones_row[:, :], 1.0).then_inc(s_const, 1)
            pool.iota(lane[:, :], pattern=[[-1, E]], base=E, channel_multiplier=0,
                      allow_small_or_imprecise_dtypes=True).then_inc(s_const, 1)
            pool.iota(list_start[:, :], pattern=[[CAP, E]], base=0, channel_multiplier=0,
                      allow_small_or_imprecise_dtypes=True).then_inc(s_const, 1)
            pool.iota(list_next[:, :], pattern=[[CAP, E]], base=0, channel_multiplier=0,
                      allow_small_or_imprecise_dtypes=True).then_inc(s_const, 1)
            pool.iota(token_of[:, :], pattern=[[P, GT]], base=0, channel_multiplier=1,
                      allow_small_or_imprecise_dtypes=True).then_inc(s_const, 1)
            pool.iota(pad_id[:, :], pattern=[[1, BI]], base=N, channel_multiplier=BI).then_inc(s_const, 1)

            def h_lo(s, c):
                pool.wait_ge(s_hhi, s * C + (c + 1))
                pool.tensor_tensor(h_q[:, 1, c, :], h_full[:, c, :], h_q[:, 0, c, :].bitcast(F32), ALU.subtract).then_inc(s_hlo, 1)

            def q_parts(s, first, last):
                for i in range(first, last):
                    pool.wait_ge(s_qr, s * ST + (i + 1))
                    qe = q_exp[:, i % 2, :].rearrange("p (h d) -> p h d", d=DH)
                    pool.tensor_tensor(qe, qe, bc(q_rec[:, i % 2, :], 2, [P, 2 * J, DH]), ALU.mult).then_inc(s_qn, 1)
                    pool.wait_ge(s_qhi, s * ST + (i + 1))
                    qh = q_hl[:, bass.ds(s & 1, 1), i, :, :, :].rearrange("p a j l d -> p (a j) l d")
                    pool.tensor_tensor(qh[:, :, 1, :], q_exp[:, i % 2, :].rearrange("p (j d) -> p j d", d=P),
                                       qh[:, :, 0, :].bitcast(F32), ALU.subtract).then_inc(s_qlo, 1)

            pool.wait_ge(s_whqk, 1)
            pool.tensor_tensor(wqk_lo[:, :, 0:HD], wqk_raw[:, :, 0:HD], wqk_hi[:, :, 0:HD].bitcast(F32), ALU.subtract).then_inc(s_wlqk, 1)

            for c in range(C):
                h_lo(0, c)
            q_parts(0, 0, 2)
            for c in range(C):
                h_lo(1, c)
            q_parts(0, 2, ST)
            with pool.Fori(1, SBN - 1) as s:
                q_parts(s, 0, ST - 1)
                for c in range(C):
                    h_lo(s + 1, c)
                q_parts(s, ST - 1, ST)
            q_parts(SBN - 1, 0, ST)

            with pool.Fori(0, GROUPS // 2) as gg:
                for par in range(2):
                    pool.wait_ge(s_spot, gg * 2 + (par + 1 + TWO))
                    pool.sem_inc(s_turn_pool, 1)
                    for i in range(GT):
                        for k in range(2):
                            pool.indirect_dma_start(lists[:, :], bass.IndirectOffsetOnAxis(ap=spot_i[:, par, i, k:k + 1], axis=0),
                                                    rows[:, par, i, :], None).then_inc(s_list[par], 16)
                    if par == 1:
                        for q in range(2):
                            pool.wait_ge(s_list[q], gg * LISTED + LISTED)
                            pool.sem_inc(s_free[q], 1)

            for half in range(2):
                pool.wait_ge(s_x1out[half], 16 * GROUPS + CREDIT)
            pool.wait_ge(s_counts, 1)
            for i in range(BI):
                pool.dma_start(out[N + i * P:N + (i + 1) * P, :], pad[:, i, 0:D]).then_inc(s_added, 16)
            g = block_counter(pool, "g_pool")

            def expert(e, par, nb, last):
                if not last:
                    pool.wait_ge(s_whi, e * 2 + 3)
                    pool.tensor_tensor(w1_lo[1 - par][:, :, :], w1_raw[:, :, :], w1_hi[1 - par][:, :, :].bitcast(F32), ALU.subtract).then_inc(s_pool, 1)
                    pool.wait_ge(s_whi, e * 2 + 4)
                    pool.tensor_tensor(w2_lo[1 - par][:, :, :], w2_raw[:, :, :], w2_hi[1 - par][:, :, :].bitcast(F32), ALU.subtract).then_inc(s_wlo, 1)
                with pool.Fori(0, nb) as b:
                    gv = now(pool, g)
                    for i in range(BI):
                        pool.wait_ge(s_y, gv * 2 + (i + 1 + TWO))
                        pool.wait_ge(s_added, gv * 32 + (16 * i + DMA2))
                        pool.sem_inc(s_turn_pool, 1)
                        pool.indirect_dma_start(out[:, :], bass.IndirectOffsetOnAxis(ap=y_id[:, i:i + 1], axis=0),
                                                y[:, i, :], None, compute_op=ALU.add).then_inc(s_added, 16)
                    pool.reg_add(g, g, 1)

            experts(pool, g, expert)
            pool.wait_ge(s_added, now(pool, g) * 32 + DMA2)
            pool.sem_inc(s_done, 1)

        @block.scalar
        def _(act):
            act.sem_inc(s_ke, TWO)
            act.sem_inc(s_rTc, TWO)
            act.sem_inc(s_gelu, FOUR)

            def h_hi(s, c, buffers_used):
                act.wait_ge(s_xt, s * C + (c + 1))
                if buffers_used and c == 0:
                    act.wait_ge(s_q, s * ST)
                    act.wait_ge(s_hk, s * 16)
                    act.wait_ge(s_hst, s * 16)
                act.activation(h_q[:, 0, c, :], ps[:, c, :], ACT.Identity, bias=modc[:, 0, c:c + 1],
                               scale=modc[:, 1, c:c + 1])
                if buffers_used:
                    act.wait_ge(s_hlo, s * C + (c - 1))
                act.activation(h_full[:, c, :], ps[:, c, :], ACT.Identity, bias=modc[:, 0, c:c + 1],
                               scale=modc[:, 1, c:c + 1]).then_inc(s_hhi, 1)

            def q_e(s, i):
                act.wait_ge(s_qs, s * ST + (i + 1))
                act.activation(q_exp[:, i % 2, :], q_exp[:, i % 2, :], ACT.Exp, scale=SCALE).then_inc(s_qe, 1)

            def q_hi(s, i):
                act.wait_ge(s_qn, s * ST + (i + 1))
                qh = q_hl[:, bass.ds(s & 1, 1), i, :, :, :].rearrange("p a j l d -> p (a j) l d")
                act.activation(qh[:, :, 0, :], q_exp[:, i % 2, :].rearrange("p (j d) -> p j d", d=P), ACT.Copy).then_inc(s_qhi, 1)

            act.wait_ge(s_cTc, 1)
            act.activation(silu_t[:, :], silu_c[:, :], ACT.Exp, scale=-1.0).then_inc(s_silu_e, 1)
            act.wait_ge(s_modr, 1)
            for c in range(C):
                h_hi(0, c, False)
            act.wait_ge(s_wqk, 16)
            q_e(0, 0)
            q_e(0, 1)
            q_hi(0, 0)
            q_e(0, 2)
            q_hi(0, 1)
            q_e(0, 3)
            for c in range(C):
                h_hi(1, c, True)
            q_hi(0, 2)

            def body(s, more, more2):
                def k_e(j):
                    act.wait_ge(s_nm, s * J + (j + 1))
                    act.wait_ge(s_kT, s * J + (j - 1 + TWO))
                    act.activation(k_exp[:, j % 2, :], ps[:, KT + j % 2, :], ACT.Exp, bias=k_nmax[:, j:j + 1],
                                   accum_out=k_part[:, j:j + 1]).then_inc(s_ke, 1)
                    act.activation(k_alpha[:, j:j + 1], k_dm[:, j:j + 1], ACT.Exp).then_inc(s_al, 1)

                def k_h(j):
                    act.wait_ge(s_kT, s * J + (j + 1 + TWO))
                    act.wait_ge(s_ctx, s * J + (j - 1 + TWO))
                    act.activation(k_hi[:, j % 2, :, :].rearrange("p t e -> p (t e)"), ps[:, TR, :], ACT.Copy).then_inc(s_khi, 1)

                for j in range(J):
                    if j >= 1:
                        k_h(j - 1)
                    k_e(j)
                    if j == 0:
                        q_hi(s, 3)
                    if more:
                        if j == 2:
                            act.wait_ge(s_ctx, s * J + TWO)
                        for slot, step, i in ((1, q_e, 0), (2, q_e, 1), (3, q_hi, 0), (4, q_e, 2),
                                              (5, q_hi, 1), (6, q_e, 3), (7, q_hi, 2)):
                            if j == slot:
                                step(s + 1, i)
                    if more2 and j >= J - C:
                        h_hi(s + 2, j - (J - C), True)
                k_h(J - 1)

            superblocks(act, body)

            for b in range(4):
                act.wait_ge(s_cw, b + 1)
                act.activation(cw[:, 2 * b:2 * b + 2, :].rearrange("p j d -> p (j d)"), ps[:, b, :], ACT.Copy).then_inc(s_cwc, 1)

            with act.Fori(0, GROUPS // 2) as gg:
                for par in range(2):
                    for i in range(GT):
                        act.wait_ge(s_rT, gg * 2 * GT + (par * GT + i + 1))
                        act.wait_ge(s_lg, gg * 2 * GT + (par * GT + i - 1 + TWO))
                        act.activation(x1T[:, i % 2, :], ps[:, RT + i % 2, 0:D], ACT.Copy).then_inc(s_rTc, 1)
                    act.wait_ge(s_lgs, gg * 2 + (par + 1 + TWO))
                    act.activation(probs[:, :, :], probs[:, :, :], ACT.Exp).then_inc(s_pe, 1)

            act.wait_ge(s_counts, 1)
            g = block_counter(act, "g_act")

            def block_hi(n):
                act.wait_ge(s_bt, n + 1 + ONE)
                for c in range(C):
                    last = act.activation(xT_hi[:, c, :], ps[:, XTB, c * BT:(c + 1) * BT], ACT.Identity,
                                          bias=modc[:, 2, c:c + 1], scale=modc[:, 3, c:c + 1])
                last.then_inc(s_bhi, 1)

            block_hi(0)

            def expert(e, par, nb, last):
                with act.Fori(0, nb) as b:
                    gv = now(act, g)
                    for k in range(M // 2):
                        act.wait_ge(s_f1, gv * 4 + (k + 1))
                        act.wait_ge(s_hid, gv * 4 + (k + 1))
                        for m in (2 * k, 2 * k + 1):
                            ins = act.activation(hid[:, m, :], ps[:, k, (m % 2) * BT:(m % 2 + 1) * BT], ACT.Gelu_apprx_tanh,
                                                 bias=b1_col[:, bass.ds(e, 1), m])
                        ins.then_inc(s_gelu, 1)
                    block_hi(gv + 1)
                    act.reg_add(g, g, 1)

            experts(act, g, expert)

        @block.vector
        def _(dve):
            chain = Link(dve, s_dve)
            link = chain.link
            for s in (s_klo, s_acc, s_lgs, s_spot, s_y):
                dve.sem_inc(s, TWO)
            dve.sem_inc(s_hid, FOUR)
            dve.sem_inc(s_x1, FOUR)
            dve.sem_inc(s_meta, ONE)

            def inverse_root(r, v, i, t):
                link(dve.tensor_scalar(i, v.bitcast(I32), 1, None, ALU.logical_shift_right))
                link(dve.tensor_scalar(r.bitcast(I32), i, -1.0, float(0x5f3759df), ALU.mult, ALU.add))
                for _ in range(3):
                    link(dve.tensor_tensor(t, r, r, ALU.mult))
                    link(dve.tensor_tensor(t, t, v, ALU.mult))
                    link(dve.tensor_scalar(t, t, -0.5, 1.5, ALU.mult, ALU.add))
                    link(dve.tensor_tensor(r, r, t, ALU.mult))

            def variance(s):
                dve.wait_ge(s_x, s * 16 + 16)
                for t in range(ST):
                    last = dve.bn_stats(ln_s[:, t, :], x_in[:, t, :])
                chain.link_apart(last, s_turn_dve)
                if not (isinstance(s, int) and s == 0):
                    dve.wait_ge(s_xn, s)
                    dve.sem_inc(s_turn_dve, 1)
                for t in range(ST):
                    last = dve.bn_aggr(ln_a[:, t, :], ln_s[:, t, :])
                link(last)
                link(dve.tensor_scalar(ln_v[:, :], ln_a[:, :, 1], EPS, None, ALU.add))

            def normalise(s, reuse):
                inverse_root(ln_r[:, :], ln_v[:, :], ln_i[:, :], ln_t[:, :])
                if reuse:
                    dve.wait_ge(s_xt, s * C)
                for t in range(ST):
                    last = dve.tensor_scalar(xn[:, t, :], x_in[:, t, :], ln_a[:, t, 0:1], ln_r[:, t:t + 1], ALU.subtract, ALU.mult)
                last.then_inc(s_xn, 1)

            def q_a(s, i, reuse):
                dve.wait_ge(s_q, s * ST + (i + 1))
                if reuse:
                    dve.wait_ge(s_qlo, s * ST + (i - 1))
                b = (i % 2) * 2
                q = ps[:, b:b + 2, :].rearrange("p b (h d) -> p (b h) d", d=DH)
                link(dve.tensor_reduce(q_max[:, i % 2, :], q, AX, ALU.max))
                dve.tensor_tensor(q_exp[:, i % 2, :].rearrange("p (h d) -> p h d", d=DH), q,
                                  bc(q_max[:, i % 2, :], 2, [P, 2 * J, DH]), ALU.subtract).then_inc(s_qs, 1)

            def q_b(s, i):
                dve.wait_ge(s_qe, s * ST + (i + 1))
                link(dve.tensor_reduce(q_sum[:, i % 2, :], q_exp[:, i % 2, :].rearrange("p (h d) -> p h d", d=DH), AX, ALU.add))
                dve.reciprocal(q_rec[:, i % 2, :], q_sum[:, i % 2, :]).then_inc(s_qr, 1)

            variance(0)
            dve.wait_ge(s_cT, 1)
            dve.tensor_copy(b1_col[:, :, :].rearrange("p e m -> p (e m)"), ps[:, 0, 64:128])
            dve.tensor_copy(silu_c[:, :], ps[:, 0, 0:C]).then_inc(s_cTc, 1)
            dve.wait_ge(s_silu_e, 1)
            link(dve.tensor_scalar(silu_t[:, :], silu_t[:, :], 1.0, None, ALU.add))
            link(dve.reciprocal(silu_t[:, :], silu_t[:, :]))
            link(dve.tensor_tensor(silu_c[:, :], silu_c[:, :], silu_t[:, :], ALU.mult))
            dve.tensor_copy(silu_b[:, :, :], bc(silu_c[:, :], 2, [P, C, P])).then_inc(s_silu, 1)
            normalise(0, False)
            dve.memset(ctx_acc[:, :, :], 0.0)
            dve.memset(k_sum[:, :], 0.0)
            link(dve.memset(k_nmax[:, :], BIG))
            dve.wait_ge(s_mod, 1)
            link(dve.tensor_copy(modc[:, :, :].rearrange("p k c -> p (k c)"), ps[:, 1, 0:4 * C]))
            link(dve.tensor_scalar(modc[:, 1, :], modc[:, 1, :], 1.0, None, ALU.add))
            link(dve.tensor_scalar(modc[:, 3, :], modc[:, 3, :], 1.0, None, ALU.add))
            dve.tensor_copy(shift_b[:, :, :], bc(modc[:, 2, :], 2, [P, C, P])).then_inc(s_modr, 1)
            g2 = ps[:, 2, :].rearrange("p (k d) -> p k d", d=D)
            dve.tensor_scalar(gate_s[:, :, :], g2, 0.0, 2.0, ALU.is_ge, ALU.mult)
            link(dve.tensor_scalar(gate_m[:, :, :], g2, -1.0, None, ALU.mult))
            link(dve.tensor_tensor(gate_m[:, :, :], gate_m[:, :, :], g2, ALU.max))
            link(dve.tensor_scalar(gate_m[:, :, :], gate_m[:, :, :], 0.25, None, ALU.max))
            link(dve.scalar_tensor_tensor(gates[:, :, :], gate_s[:, :, :], 1.0, gate_m[:, :, :], ALU.subtract, ALU.mult))
            dve.wait_ge(s_wqk, 16)
            dve.tensor_copy(wqk_hi[:, :, 0:HD], wqk_raw[:, :, 0:HD]).then_inc(s_whqk, 1)
            dve.tensor_copy(wqk_hi[:, :, HD:2 * HD], wqk_raw[:, :, HD:2 * HD]).then_inc(s_whqk, 1)
            dve.wait_ge(s_whqk, 2)
            dve.tensor_tensor(wqk_lo[:, :, HD:2 * HD], wqk_raw[:, :, HD:2 * HD], wqk_hi[:, :, HD:2 * HD].bitcast(F32), ALU.subtract).then_inc(s_wlqk, 1)
            dve.wait_ge(s_small, 48)
            link(dve.tensor_tensor(bo_bc[:, :], bo_bc[:, :], gates[:, 0, :], ALU.mult))
            dve.tensor_tensor(wg_mod[:, :, :], wg_raw[:, :, :], bc(modc[:, 3, :], 2, [P, C, E]), ALU.mult)
            dve.wait_ge(s_bgp, 1)
            dve.tensor_tensor(bg_bc[:, :], bg_bc[:, :], ps[:, 3, 0:E], ALU.add).then_inc(s_bgr, 1)
            for half in range(2):
                dve.wait_ge(s_wvT, half + 1)
                dve.tensor_copy(wvT[:, 4 * half:4 * half + 4, :], ps[:, 4 + 2 * half:6 + 2 * half, :].rearrange("p b (j f) -> p (b j) f", f=D)).then_inc(s_wvTc, 1)

            variance(1)
            q_a(0, 0, False)
            normalise(1, True)
            q_a(0, 1, False)
            q_b(0, 0)
            q_a(0, 2, True)
            q_b(0, 1)
            q_a(0, 3, True)
            q_b(0, 2)
            q_b(0, 3)
            dve.wait_ge(s_wlqk, 2)
            dreg = dve.alloc_register("dve_chain")
            chain.enter(dreg)

            def body(s, more, more2):
                def k_m(j):
                    dve.wait_ge(s_kt, s * J + (j + 1))
                    link(dve.tensor_reduce(k_blk[:, j:j + 1], ps[:, KT + j % 2, :], AX, ALU.max, negate=True))
                    link(dve.scalar_tensor_tensor(k_dm[:, j:j + 1], k_blk[:, j:j + 1], k_nmax[:, j:j + 1], k_nmax[:, j:j + 1], ALU.min, ALU.subtract))
                    dve.tensor_tensor(k_nmax[:, j:j + 1], k_nmax[:, j:j + 1], k_blk[:, j:j + 1], ALU.min).then_inc(s_nm, 1)

                def k_l(j):
                    dve.wait_ge(s_khi, s * J + (j + 1))
                    dve.tensor_tensor(k_lo[:, j % 2, :, :].rearrange("p t e -> p (t e)"), ps[:, TR, :],
                                      k_hi[:, j % 2, :, :].rearrange("p t e -> p (t e)").bitcast(F32), ALU.subtract).then_inc(s_klo, 1)

                def acc(j):
                    dve.wait_ge(s_ctx, s * J + (j + 1 + TWO))
                    dve.wait_ge(s_al, s * J + (j + 1))
                    dve.wait_ge(s_acc, s * J + (j + TWO))
                    al = k_alpha[:, j:j + 1]
                    dve.scalar_tensor_tensor(k_sum[:, j:j + 1], k_sum[:, j:j + 1], al, k_part[:, j:j + 1], ALU.mult, ALU.add)
                    link(dve.scalar_tensor_tensor(ctx_t[:, :], ctx_acc[:, j, :], al, ps[:, CX, 0:P], ALU.mult, ALU.add))
                    dve.tensor_tensor(ctx_acc[:, j, :], ctx_t[:, :], ps[:, CX, P:2 * P], ALU.add).then_inc(s_acc, 1)

                for j in range(J):
                    k_m(j)
                    if j >= 1:
                        k_l(j - 1)
                    if j >= 2:
                        acc(j - 2)
                    if more:
                        for slot, step in ((0, lambda: q_a(s + 1, 0, True)), (1, lambda: q_a(s + 1, 1, True)),
                                           (2, lambda: q_b(s + 1, 0)), (3, lambda: q_b(s + 1, 1)),
                                           (3, lambda: q_a(s + 1, 2, True)), (5, lambda: q_b(s + 1, 2)),
                                           (5, lambda: q_a(s + 1, 3, True)), (7, lambda: q_b(s + 1, 3))):
                            if j == slot:
                                step()
                    if more2:
                        if j == 3:
                            variance(s + 2)
                        if j == 5:
                            normalise(s + 2, True)
                k_l(J - 1)
                acc(J - 2)
                acc(J - 1)
                if not isinstance(s, int) or more:
                    chain.end()
                    chain.begin()

            with dve.Fori(0, SBN - 2) as s:
                chain.begin()
                body(s, True, True)
            chain.begin()
            body(SBN - 2, True, False)
            body(SBN - 1, False, False)

            dve.wait_ge(s_acc, SBN * J + TWO)
            dve.wait_ge(s_khi, SBN * J)
            dve.wait_ge(s_qlo, TILES)
            dve.wait_ge(s_hk, 16 * SBN)
            dve.wait_ge(s_hst, 16 * SBN)
            dve.memset(ctx_n[:, :, :], 0.0)
            link(dve.reciprocal(k_rec[:, :], k_sum[:, :]))
            for h in range(2):
                r = slice(h * DH, (h + 1) * DH)
                last = dve.tensor_tensor(ctx_n[r, :, r], ctx_acc[r, :, r], bc(k_rec[r, :], 2, [DH, J, DH]), ALU.mult)
            last.then_inc(s_ctxn, 1)
            dve.memset(chosen_bf[:, GT:GT + 1, :], 0.0)
            link(dve.memset(pad[:, :, :], 0.0))
            dve.wait_ge(s_const, 9)
            dve.tensor_copy(pad[:, :, ROW - 1].bitcast(I32), pad_id[:, :]).then_inc(s_pad, 1)
            dve.sem_inc(s_pad, 1)
            dve.wait_ge(s_fold, 1)
            link(dve.tensor_tensor(fold[:, :, :], ps[:, 4:6, 0:D], bc(gates[:, 0, :], 1, [P, C, D]), ALU.mult))
            link(dve.tensor_copy(fold_hi[:, :, :], fold[:, :, :]))
            dve.tensor_tensor(fold_lo[:, :, :], fold[:, :, :], fold_hi[:, :, :].bitcast(F32), ALU.subtract).then_inc(s_foldr, 1)

            def tiles(gg, par):
                t0 = gg * 2 * GT + par * GT
                for n in range(GT // 2):
                    two = slice(2 * n, 2 * n + 2)
                    if n % 2 == 0:
                        dve.wait_ge(s_x1out[n // 2], gg * 32 + (16 * par + CREDIT))
                    dve.wait_ge(s_at, t0 + (2 * n + 2))
                    dve.tensor_tensor(x1[:, two, :], ps[:, AT + n % 2, :].rearrange("p (i d) -> p i d", d=D),
                                      x_b[:, par, two, :], ALU.add).then_inc(s_x1, 2)
                    if n:
                        dve.wait_ge(s_x1, t0 + (2 * n + FOUR))
                        for i in (2 * n - 2, 2 * n - 1):
                            dve.bn_stats(bn_s[:, i, :], x1[:, i, :])
                dve.wait_ge(s_x1, t0 + (GT + FOUR))
                for i in (GT - 2, GT - 1):
                    last = dve.bn_stats(bn_s[:, i, :], x1[:, i, :])
                chain.link_apart(last, s_turn_dve)
                for i in range(GT):
                    last = dve.bn_aggr(bn_a[:, i, :], bn_s[:, i, :])
                link(last)
                link(dve.tensor_scalar(bn_v[:, :], bn_a[:, :, 1], EPS, None, ALU.add))
                inverse_root(bn_r[:, :], bn_v[:, :], bn_i[:, :], bn_t[:, :])
                for i in range(GT):
                    dve.tensor_scalar(rows[:, par, i, 0:D], x1[:, i, :], bn_a[:, i, 0:1], bn_r[:, i:i + 1], ALU.subtract, ALU.mult).then_inc(s_row, 1)

            def route(gg, par):
                shape = [P, GT, E]
                g = gg * 2 + par
                dve.wait_ge(s_lg, (g + 1) * GT + TWO)
                link(dve.tensor_tensor(probs[:, :, :], ps[:, LG + par, 0:GT * E].rearrange("p (t e) -> p t e", e=E),
                                       bc(bg_bc[:, :], 1, shape), ALU.add))
                link(dve.tensor_reduce(red[:, :], probs[:, :, :], AX, ALU.max))
                dve.tensor_tensor(probs[:, :, :], probs[:, :, :], bc(red[:, :], 2, shape), ALU.subtract).then_inc(s_lgs, 1)
                dve.wait_ge(s_pe, g + 1)
                link(dve.tensor_reduce(red[:, :], probs[:, :, :], AX, ALU.add))
                link(dve.reciprocal(red[:, :], red[:, :]))
                link(dve.tensor_tensor(probs[:, :, :], probs[:, :, :], bc(red[:, :], 2, shape), ALU.mult))
                for k, p in ((0, probs), (1, rest)):
                    link(dve.tensor_reduce(red[:, :], p[:, :, :], AX, ALU.max))
                    link(dve.tensor_tensor(cand[:, :, :], p[:, :, :], bc(red[:, :], 2, shape), ALU.is_equal))
                    link(dve.tensor_tensor(cand[:, :, :], cand[:, :, :], bc(lane[:, :], 1, shape), ALU.mult))
                    link(dve.tensor_reduce(red[:, :], cand[:, :, :], AX, ALU.max))
                    link(dve.tensor_tensor(pick[:, k, :, :], cand[:, :, :], bc(red[:, :], 2, shape), ALU.is_equal))
                    if k == 0:
                        link(dve.scalar_tensor_tensor(rest[:, :, :], pick[:, 0, :, :], -4.0, probs[:, :, :], ALU.mult, ALU.add))
                link(dve.tensor_tensor(chosen[:, :, :], pick[:, 0, :, :], pick[:, 1, :, :], ALU.add))
                dve.tensor_copy(chosen_bf[:, 0:GT, :], chosen[:, :, :]).then_inc(s_ch, 1)
                dve.wait_ge(s_ch, g + 1)
                link(dve.tensor_tensor(chosen[:, :, :], probs[:, :, :], chosen[:, :, :], ALU.mult))
                link(dve.tensor_reduce(red[:, :], chosen[:, :, :], AX, ALU.add))
                link(dve.tensor_scalar(red[:, :], red[:, :], 1e-8, None, ALU.add))
                link(dve.reciprocal(red[:, :], red[:, :]))
                dve.tensor_tensor(rows[:, par, :, D:D + E], chosen[:, :, :], bc(red[:, :], 2, shape), ALU.mult)
                link(dve.tensor_copy(rows[:, par, :, ROW - 1].bitcast(I32), token_of[:, :]))
                link(dve.tensor_scalar(token_of[:, :], token_of[:, :], float(GT * P), None, ALU.add))
                dve.wait_ge(s_rk, g + 1)
                link(dve.tensor_tensor(spot[:, :, :], ps[:, RK + par, 0:GT * E].rearrange("p (t e) -> p t e", e=E),
                                       bc(list_next[:, :], 1, shape), ALU.add))
                link(dve.tensor_tensor(list_next[:, :], list_next[:, :], ps[:, RK + par, GT * E:(GT + 1) * E], ALU.add))
                for k in range(2):
                    link(dve.tensor_tensor(cand[:, :, :], spot[:, :, :], pick[:, k, :, :], ALU.mult))
                    link(dve.tensor_reduce(spot_k[:, k, :], cand[:, :, :], AX, ALU.add))
                dve.tensor_copy(spot_i[:, par, :, :].rearrange("p t k -> p k t"), spot_k[:, :, :]).then_inc(s_spot, 1)

            chain.end()
            with dve.Fori(0, GROUPS // 2) as gg:
                for par in range(2):
                    chain.begin()
                    dve.wait_ge(s_xb[par], gg * 16 + 16)
                    dve.wait_ge(s_free[par], gg + 1)
                    tiles(gg, par)
                    route(gg, par)
                    chain.end()
            chain.begin()

            dve.wait_ge(s_b2, 16)
            dve.tensor_tensor(b2_bc[:, :, :], b2_bc[:, :, :], bc(gates[:, 1, :], 1, [P, E, D]), ALU.mult)

            def w_hi(par):
                dve.tensor_copy(w1_hi[par][:, :, :], w1_raw[:, :, :]).then_inc(s_whi, 1)
                link(dve.tensor_tensor(w2_raw[:, :, :], w2_raw[:, :, :], bc(gates[:, 1, :], 1, [P, M, D]), ALU.mult))
                dve.tensor_copy(w2_hi[par][:, :, :], w2_raw[:, :, :]).then_inc(s_whi, 1)

            link(dve.tensor_tensor(counts_f[:, :], list_next[:, :], list_start[:, :], ALU.subtract))
            link(dve.tensor_copy(counts[:, :], counts_f[:, :]))
            link(dve.tensor_scalar(counts_f[:, :], counts_f[:, :], float(BT - 1), None, ALU.add))
            link(dve.tensor_copy(blocks[:, :], counts_f[:, :]))
            link(dve.tensor_scalar(blocks[:, :], blocks[:, :], BT.bit_length() - 1, None, ALU.arith_shift_right))
            link(dve.tensor_scalar(blocks[:, :], blocks[:, :], 1, None, ALU.max))
            dve.sem_inc(s_counts, 1)
            dve.wait_ge(s_wraw, 32)
            w_hi(0)
            dve.wait_ge(s_whi, 2)
            dve.tensor_tensor(w1_lo[0][:, :, :], w1_raw[:, :, :], w1_hi[0][:, :, :].bitcast(F32), ALU.subtract)
            dve.tensor_tensor(w2_lo[0][:, :, :], w2_raw[:, :, :], w2_hi[0][:, :, :].bitcast(F32), ALU.subtract).then_inc(s_wlo, 1)

            g = block_counter(dve, "g_dve")
            for par in range(2):
                dve.wait_ge(s_list[par], G_END)
                dve.wait_ge(s_x1out[par], 16 * GROUPS + CREDIT)

            def block_lo(n):
                dve.wait_ge(s_bhi, n + 1)
                if not isinstance(n, int):
                    dve.wait_ge(s_blo, n)
                for c in range(C):
                    last = dve.tensor_scalar(xT_full[:, c, :], ps[:, XTB, c * BT:(c + 1) * BT], modc[:, 3, c:c + 1],
                                             modc[:, 2, c:c + 1], ALU.mult, ALU.add)
                link(last)
                dve.tensor_tensor(xT_lo[:, :, :], xT_full[:, :, :], xT_hi[:, :, :].bitcast(F32), ALU.subtract).then_inc(s_blo, 1)

            block_lo(0)
            chain.end()

            def expert(e, par, nb, last_expert):
                if not last_expert:
                    chain.begin()
                    dve.wait_ge(s_wraw, e * 32 + 64)
                    dve.wait_ge(s_f2, now(dve, g) * 2 + TWO)
                    w_hi(1 - par)
                    chain.end()
                with dve.Fori(0, nb) as b:
                    chain.begin()
                    gv = now(dve, g)
                    for k in range(M // 2):
                        dve.wait_ge(s_gelu, gv * 4 + (k + 1 + FOUR))
                        if k == 0:
                            dve.wait_ge(s_f2, gv * 2 + TWO)
                        m = slice(2 * k, 2 * k + 2)
                        link(dve.tensor_copy(hid_hi[:, m, :], hid[:, m, :]))
                        dve.tensor_tensor(hid_lo[:, m, :], hid[:, m, :], hid_hi[:, m, :].bitcast(F32), ALU.subtract).then_inc(s_hid, 1)
                        if k == 0:
                            dve.wait_ge(s_rows, gv * 16 + 16)
                            dve.wait_ge(s_added, gv * 32 + DMA2)
                            dve.tensor_copy(y_w[:, :, :], listed[:, :, D:D + E])
                            dve.tensor_copy(y_id[:, :], listed[:, :, ROW - 1].bitcast(I32)).then_inc(s_meta, 1)

                    def rows_out(i):
                        dve.wait_ge(s_f2, gv * 2 + (i + 1 + TWO))
                        dve.wait_ge(s_added, gv * 32 + (16 * i + 16))
                        link(dve.tensor_tensor(y[:, i, :], ps[:, Y0 + i, 0:D], b2_bc[:, bass.ds(e, 1), :].rearrange("p a d -> p (a d)"), ALU.add))
                        dve.tensor_scalar(y[:, i, :], y[:, i, :], y_w[:, i, bass.ds(e, 1)], None, ALU.mult).then_inc(s_y, 1)

                    rows_out(0)
                    block_lo(gv + 1)
                    rows_out(1)
                    chain.end()
                    dve.reg_add(g, g, 1)

            experts(dve, g, expert)

        @block.tensor
        def _(pe):
            for s in (s_kT, s_ctx, s_lg, s_f2):
                pe.sem_inc(s, TWO)
            pe.sem_inc(s_bt, ONE)

            pe.wait_ge(s_const, 1)
            pe.wait_ge(s_c, 32)
            pe.transpose(ps[:, 0, 0:C], c_rows[:, :], ident[0:C, 0:C])
            pe.transpose(ps[:, 0, 64:64 + E * M], b1_rows[:, :], ident[0:E * M, 0:E * M]).then_inc(s_cT, 1)
            pe.wait_ge(s_silu, 1)
            pe.wait_ge(s_wmod, 16)
            for n, k in enumerate((0, 1, 3, 4)):
                for c2 in range(C):
                    for c in range(C):
                        pe.matmul(ps[:, 1, n * C + c2:n * C + c2 + 1], wmod_sb[:, c, k * D + c2 * P:k * D + (c2 + 1) * P],
                                  silu_c[:, c:c + 1], start=c == 0, stop=c == C - 1)
            for n, k in enumerate((2, 5)):
                for c in range(C):
                    last = pe.matmul(ps[:, 2, n * D:(n + 1) * D], silu_b[:, c, :], wmod_sb[:, c, k * D:(k + 1) * D],
                                     start=c == 0, stop=c == C - 1)
            last.then_inc(s_mod, 1)

            def x_T(s, c, reuse):
                pe.wait_ge(s_xn, s + 1)
                if reuse:
                    pe.wait_ge(s_qs, s * ST - 1)
                for t in range(ST):
                    last = pe.transpose(ps[:, c, t * P:(t + 1) * P], xn[:, t, c * P:(c + 1) * P], ident[:, :])
                last.then_inc(s_xt, 1)

            def q_mm(s, i, reuse):
                if i == 0:
                    pe.wait_ge(s_hlo, s * C + C)
                if reuse:
                    pe.wait_ge(s_qs, s * ST + (i - 1))
                b = (i % 2) * 2
                tok = slice(i * P, (i + 1) * P)
                for half in range(2):
                    col = slice(half * 512, (half + 1) * 512)
                    for a, w, st, sp_ in three([((h_q[:, 0, c, tok], h_q[:, 1, c, tok]), (wqk_hi[:, c, col], wqk_lo[:, c, col])) for c in range(C)]):
                        last = pe.matmul(ps[:, b + half, :], a, w, start=st, stop=sp_)
                last.then_inc(s_q, 1)

            pe.wait_ge(s_cTc, 1)
            x_T(0, 0, False)
            pe.wait_ge(s_modr, 1)
            x_T(0, 1, False)
            pe.wait_ge(s_small, 48)
            for c in range(C):
                last = pe.matmul(ps[:, 3, 0:E], shift_b[:, c, :], wg_raw[:, c, :], start=c == 0, stop=c == C - 1)
            last.then_inc(s_bgp, 1)
            pe.wait_ge(s_fold_in, 32)
            for half in range(2):
                for j in range(4 * half, 4 * half + 4):
                    for c in range(C):
                        last = pe.transpose(ps[:, 4 + j // 2, (j % 2) * D + c * P:(j % 2) * D + (c + 1) * P],
                                            wv_raw[:, c, j * P:(j + 1) * P], ident[:, :])
                last.then_inc(s_wvT, 1)
            pe.wait_ge(s_wlqk, 2)
            pe.wait_ge(s_bgr, 1)
            for i in range(ST):
                q_mm(0, i, i >= 2)
            for c in range(C):
                x_T(1, c, True)
            pe.wait_ge(s_wvTc, 2)

            def body(s, more, more2):
                def k_mm(j):
                    if j == 0:
                        pe.wait_ge(s_hk, s * 16 + 16)
                    pe.wait_ge(s_ke, s * J + (j - 1 + TWO))
                    col = slice(HD + j * P, HD + (j + 1) * P)
                    hk = [[h_k[:, bass.ds(s & 1, 1), l, c, :].rearrange("p a t -> p (a t)") for l in range(2)] for c in range(C)]
                    for w, a, st, sp_ in three([((wqk_hi[:, c, col], wqk_lo[:, c, col]), hk[c]) for c in range(C)]):
                        last = pe.matmul(ps[:, KT + j % 2, :], w, a, start=st, stop=sp_)
                    last.then_inc(s_kt, 1)

                def k_T(j):
                    pe.wait_ge(s_ke, s * J + (j + 1 + TWO))
                    pe.wait_ge(s_klo, s * J + (j + TWO))
                    for t in range(ST):
                        last = pe.transpose(ps[:, TR, t * P:(t + 1) * P], k_exp[:, j % 2, t * P:(t + 1) * P], ident[:, :])
                    last.then_inc(s_kT, 1)

                def c_mm(j):
                    if j == 0:
                        pe.wait_ge(s_qlo, s * ST + ST)
                    pe.wait_ge(s_klo, s * J + (j + 1 + TWO))
                    pe.wait_ge(s_acc, s * J + (j + TWO))
                    for t in range(ST):
                        q = q_hl[:, bass.ds(s & 1, 1), t, j, :, :].rearrange("p a l d -> p (a l d)")
                        for n, kk in enumerate((k_hi, k_lo)):
                            last = pe.matmul(ps[:, CX, 0:2 * P], kk[:, j % 2, t, :], q, start=t == 0 and n == 0, stop=t == ST - 1 and n == 1)
                    last.then_inc(s_ctx, 1)

                for j in range(J):
                    k_mm(j)
                    if j >= 1:
                        k_T(j - 1)
                    if j >= 2:
                        c_mm(j - 2)
                    if more:
                        for slot, i in ((0, 0), (1, 1), (3, 2), (5, 3)):
                            if j == slot:
                                q_mm(s + 1, i, True)
                    if more2 and j >= J - C:
                        x_T(s + 2, j - (J - C), True)
                k_T(J - 1)
                c_mm(J - 2)
                c_mm(J - 1)

            superblocks(pe, body)

            pe.wait_ge(s_ctxn, 1)
            for j in range(J):
                last = pe.matmul(ps[:, j // 2, (j % 2) * D:(j % 2 + 1) * D], ctx_n[:, j, :], wout_sb[:, j, :], start=True, stop=True)
                if j % 2:
                    last.then_inc(s_cw, 1)
            for c in range(C):
                for j in range(J):
                    pe.wait_ge(s_cwc, j // 2 + 1)
                    last = pe.matmul(ps[:, 4 + c, 0:D], wvT[:, j, c * P:(c + 1) * P], cw[:, j, :], start=j == 0, stop=j == J - 1)
            last.then_inc(s_fold, 1)
            pe.wait_ge(s_foldr, 1)

            def attend(gg, par, n):
                t = gg * 2 * GT + (par * GT + 2 * n)
                if n == 0:
                    pe.wait_ge(s_hb[par], gg * 64 + 64)
                pe.wait_ge(s_x1, t - 2 + FOUR)
                for i in (2 * n, 2 * n + 1):
                    tok = slice((i % ST) * P, (i % ST + 1) * P)
                    h = h_b[:, par, :, i // ST, :, :]
                    o = ps[:, AT + n % 2, (i % 2) * D:(i % 2 + 1) * D]
                    for a, w, st, _ in three([((h[:, 0, c, tok], h[:, 1, c, tok]), (fold_hi[:, c, :], fold_lo[:, c, :])) for c in range(C)]):
                        pe.matmul(o, a, w, start=st, stop=False)
                    last = pe.matmul(o, ones_row[0:1, :], bo_bc[0:1, :], start=False, stop=True)
                last.then_inc(s_at, 2)

            with pe.Fori(0, GROUPS // 2) as gg:
                for par in range(2):
                    for n in range(GT // 2):
                        attend(gg, par, n)
                    for i in range(GT):
                        t = gg * 2 * GT + (par * GT + i)
                        pe.wait_ge(s_row, t + 1)
                        pe.wait_ge(s_rTc, t - 1 + TWO)
                        for c in range(C):
                            last = pe.transpose(ps[:, RT + i % 2, c * P:(c + 1) * P], rows[:, par, i, c * P:(c + 1) * P], ident[:, :])
                        last.then_inc(s_rT, 1)
                        pe.wait_ge(s_rTc, t + 1 + TWO)
                        if i == 0:
                            pe.wait_ge(s_lgs, gg * 2 + (par - 1 + TWO))
                        for c in range(C):
                            last = pe.matmul(ps[:, LG + par, i * E:(i + 1) * E], x1T[:, i % 2, c * P:(c + 1) * P], wg_mod[:, c, :],
                                             start=c == 0, stop=c == C - 1)
                        last.then_inc(s_lg, 1)
                    pe.wait_ge(s_ch, gg * 2 + (par + 1))
                    pe.wait_ge(s_spot, gg * 2 + (par - 1 + TWO))
                    pe.matmul(ps[:, RK + par, 0:(GT + 1) * E], before_bf[:, :], chosen_bf[:, :, :], start=True, stop=False)
                    for i in range(GT):
                        last = pe.matmul(ps[:, RK + par, (i + 1) * E:(GT + 1) * E], ones_bf[:, :],
                                         bc(chosen_bf[:, i, :], 1, [P, GT - i, E]), start=False, stop=i == GT - 1)
                    last.then_inc(s_rk, 1)

            pe.wait_ge(s_counts, 1)
            g = block_counter(pe, "g_pe")

            def block_T(n):
                pe.wait_ge(s_rows, n * 16 + 16)
                for c in range(C):
                    for i in range(BI):
                        last = pe.transpose(ps[:, XTB, c * BT + i * P:c * BT + (i + 1) * P], listed[:, i, c * P:(c + 1) * P], ident[:, :])
                last.then_inc(s_bt, 1)

            block_T(0)

            def expert(e, par, nb, last_expert):
                pe.wait_ge(s_wlo, e + 1)
                pe.sem_inc(s_turn_pe, 1)
                with pe.Fori(0, nb) as b:
                    gv = now(pe, g)
                    pe.wait_ge(s_blo, gv + 1)
                    for m in range(M):
                        k = m // 2
                        if m % 2 == 0:
                            pe.wait_ge(s_gelu, gv * 4 + (k + 1))
                        col = slice(m * P, (m + 1) * P)
                        for w, a, st, sp_ in three([((w1_hi[par][:, c, col], w1_lo[par][:, c, col]), (xT_hi[:, c, :], xT_lo[:, c, :])) for c in range(C)]):
                            last = pe.matmul(ps[:, k, (m % 2) * BT:(m % 2 + 1) * BT], w, a, start=st, stop=sp_)
                        if m % 2:
                            last.then_inc(s_f1, 1)

                    def second(i):
                        pe.wait_ge(s_y, gv * 2 + (i + 1))
                        r = slice(i * P, (i + 1) * P)
                        for m in range(M):
                            if i == 0 and m % 2 == 0:
                                pe.wait_ge(s_hid, gv * 4 + (m // 2 + 1 + FOUR))
                            for a, w, st, sp_ in three([((hid_hi[:, m, r], hid_lo[:, m, r]), (w2_hi[par][:, m, :], w2_lo[par][:, m, :]))]):
                                last = pe.matmul(ps[:, Y0 + i, 0:D], a, w, start=m == 0 and st, stop=m == M - 1 and sp_)
                        last.then_inc(s_f2, 1)

                    second(0)
                    block_T(gv + 1)
                    second(1)
                    pe.reg_add(g, g, 1)

            experts(pe, g, expert)


_INS = ['L0_attn_x', 'L0_attn_w_qkv', 'L0_attn_w_out', 'L0_attn_b_out', 'L0_ffn_Wg', 'L0_ffn_bg', 'L0_ffn_W1',
        'L0_ffn_b1', 'L0_ffn_W2', 'L0_ffn_b2', 'L0_c', 'L0_wmod']


def kernel(**inputs):
    import numpy as _np
    import concourse.bacc as _bacc
    from concourse import mybir as _mybir
    from concourse.bass_utils import run_bass_kernel_spmd as _run

    nc = _bacc.Bacc("TRN2", target_bir_lowering=False, num_devices=1)
    arrays, args = {}, []
    for name in _INS:
        a = _np.ascontiguousarray(inputs[name])
        arrays[f"in_{name}"] = a
        args.append(nc.dram_tensor(f"in_{name}", a.shape, _mybir.dt.from_np(a.dtype), kind="ExternalInput").ap())
    args.append(nc.dram_tensor("out", (N + BT, D), _mybir.dt.float32, kind="ExternalOutput").ap())
    adaln_block(nc, *args)
    r = _run(nc, [arrays], core_ids=[0])
    return r.results[0]["out"][:N].reshape(1, N, D)
```

```python
from contextlib import ExitStack

import concourse.bass as bass
from concourse import mybir

F32 = mybir.dt.float32
F32R = mybir.dt.float32r
BF16 = mybir.dt.bfloat16
I32 = mybir.dt.int32
ALU = mybir.AluOpType
ACT = mybir.ActivationFunctionType
AX = mybir.AxisListType.X

P = 128
N = 4096
D = 256
C = D // P
HD = 1024
J = HD // P
DH = 64
TILES = N // P
ST = 4
SBN = TILES // ST
STOK = ST * P
E = 8
FH = 1024
M = FH // P
GT = 8
GROUPS = TILES // GT
RB = 3
BT = 256
BI = BT // P
CAP = N + BT
ROW = D + E + 1
MAXB = N // BT
EPS = 1e-5
SCALE = DH ** -0.5
BIG = 3.0e38


def bc(ap, axis, shape):
    return ap.unsqueeze(axis).to_broadcast(shape)


class Link:

    def __init__(self, eng, sem):
        self.eng, self.sem, self.base, self.n = eng, sem, 0, 0

    def link(self, ins):
        self.n += 1
        ins.then_inc(self.sem, 1)
        self.eng.wait_ge(self.sem, self.base + self.n)

    def link_apart(self, ins, turn):
        self.link(ins)
        self.eng.sem_inc(turn, 1)

    def enter(self, reg):
        self.reg = reg
        self.eng.reg_mov(reg, self.base + self.n)
        self.begin()

    def begin(self):
        self.n = 0
        self.base = self.eng.snap(self.reg, min_val=0, max_val=60000)

    def end(self):
        self.eng.reg_add(self.reg, self.reg, self.n)
        self.n = 0


def adaln_block(nc, x, w_qkv, w_out, b_out, Wg, bg, W1, b1, W2, b2, cvec, wmod, out):
    ctx = ExitStack()
    with ctx:
        def sb(name, shape, dt, stack=ctx):
            return stack.enter_context(nc.sbuf_tensor(name, shape, dt))

        def sem(name):
            return ctx.enter_context(nc.semaphore(name))

        ps = ctx.enter_context(nc.psum_tensor("ps", [P, 8, 512], F32))

        ident = sb("ident", [P, P], F32)
        before_bf = sb("before_bf", [P, P], BF16)
        ones_bf = sb("ones_bf", [P, P], BF16)
        lane = sb("lane", [P, E], F32)
        list_start = sb("list_start", [P, E], F32)
        list_next = sb("list_next", [P, E], F32)
        token_of = sb("token_of", [P, GT], F32)
        ones_row = sb("ones_row", [1, P], F32)
        silu_c = sb("silu_c", [P, C], F32)
        silu_t = sb("silu_t", [P, C], F32)
        silu_b = sb("silu_b", [P, C, P], F32)
        modc = sb("modc", [P, 4, C], F32)
        shift_b = sb("shift_b", [P, C, P], F32)
        gates = sb("gates", [P, 2, D], F32)
        gate_s = sb("gate_s", [P, 2, D], F32)
        gate_m = sb("gate_m", [P, 2, D], F32)
        bo_bc = sb("bo_bc", [P, D], F32)
        bo_hl = sb("bo_hl", [1, 2, 2, D], F32R)
        ones_r = sb("ones_r", [1, P], F32R)
        wg_raw = sb("wg_raw", [P, C, E], F32)
        wg_mod = sb("wg_mod", [P, C, E], F32)
        bg_bc = sb("bg_bc", [P, E], F32)
        b1_rows = sb("b1_rows", [E * M, P], F32)
        b1_col = sb("b1_col", [P, E, M], F32)
        c_rows = sb("c_rows", [C, P], F32)
        counts_f = sb("counts_f", [P, E], F32)
        counts = sb("counts", [P, E], I32)
        blocks = sb("blocks", [P, E], I32)
        pad_id = sb("pad_id", [P, BI], I32)
        listed_w = sb("listed_w", [P, BI, E], F32)
        listed_id = sb("listed_id", [P, BI], I32)
        y_w = sb("y_w", [P, BI, E], F32)
        y_id = sb("y_id", [P, BI], I32)
        ctx_acc = sb("ctx_acc", [P, J, 2 * P], F32)
        k_sum = sb("k_sum", [P, J], F32)
        k_rec = sb("k_rec", [P, J], F32)
        wv_raw = sb("wv_raw", [P, C, HD], F32)
        wvT = sb("wvT", [P, J, D], F32)
        wout_sb = sb("wout_sb", [P, J, D], F32)

        a_stack = ExitStack()
        wqk_hi = sb("wqk_hi", [P, C, 2 * HD], F32R, a_stack)
        wqk_lo = sb("wqk_lo", [P, C, 2 * HD], F32R, a_stack)
        x_in = sb("x_in", [P, ST, D], F32, a_stack)
        xn = sb("xn", [P, ST, D], F32, a_stack)
        ln_s = sb("ln_s", [P, ST, 6], F32, a_stack)
        ln_a = sb("ln_a", [P, ST, 2], F32, a_stack)
        ln_v = sb("ln_v", [P, ST], F32, a_stack)
        ln_i = sb("ln_i", [P, ST], I32, a_stack)
        ln_t = sb("ln_t", [P, ST], F32, a_stack)
        ln_r = sb("ln_r", [P, ST], F32, a_stack)
        ln_b = sb("ln_b", [P, ST], F32, a_stack)
        h_full = sb("h_full", [P, C, STOK], F32, a_stack)
        h_q = sb("h_q", [P, 2, C, STOK], F32R, a_stack)
        h_k = sb("h_k", [P, 2, 2, C, STOK], F32R, a_stack)
        k_exp = sb("k_exp", [P, 2, STOK], F32, a_stack)
        k_hi = sb("k_hi", [P, 2, ST, P], F32R, a_stack)
        k_lo = sb("k_lo", [P, 2, ST, P], F32R, a_stack)
        q_exp = sb("q_exp", [P, 2, HD], F32, a_stack)
        q_max = sb("q_max", [P, 2, 2 * J], F32, a_stack)
        q_sum = sb("q_sum", [P, 2, 2 * J], F32, a_stack)
        q_rec = sb("q_rec", [P, 2, 2 * J], F32, a_stack)
        k_blk = sb("k_blk", [P, J], F32, a_stack)
        k_nmax = sb("k_nmax", [P, J], F32, a_stack)
        k_new = sb("k_new", [P, J], F32, a_stack)
        k_alpha = sb("k_alpha", [P, J], F32, a_stack)
        k_part = sb("k_part", [P, J], F32, a_stack)
        setup_stack = ExitStack()
        wqk_raw = sb("wqk_raw", [P, C, 2 * HD], F32, setup_stack)
        wmod_sb = sb("wmod_sb", [P, C, 6 * D], F32, setup_stack)
        setup_stack.close()
        q_hl = sb("q_hl", [P, 2, ST, J, 2, P], F32R, a_stack)
        a_stack.close()

        b_stack = ExitStack()
        w1_hi = [sb("w1_hi0", [P, C, FH], F32R, b_stack)]
        w1_lo = [sb("w1_lo0", [P, C, FH], F32R, b_stack)]
        w2_hi = [sb("w2_hi0", [P, M, D], F32R, b_stack)]
        w2_lo = [sb("w2_lo0", [P, M, D], F32R, b_stack)]
        w1_raw = sb("w1_raw", [P, C, FH], F32, b_stack)
        w2_raw = sb("w2_raw", [P, M, D], F32, b_stack)
        b2_bc = sb("b2_bc", [P, E, D], F32, b_stack)
        listed = sb("listed", [P, BI, ROW], F32, b_stack)
        pad = sb("pad", [P, BI, ROW], F32, b_stack)
        bb_stack = ExitStack()
        fold_stack = ExitStack()
        ctx_n = sb("ctx_n", [P, J, P], F32, fold_stack)
        cw = sb("cw", [P, J, D], F32, fold_stack)
        fold_stack.close()
        rows = sb("rows", [P, RB, GT, ROW], F32, bb_stack)
        fold = sb("fold", [P, C, D], F32, bb_stack)
        fold_hi = sb("fold_hi", [P, C, D], F32R, bb_stack)
        fold_lo = sb("fold_lo", [P, C, D], F32R, bb_stack)
        h_b = sb("h_b", [P, 2, 2, 2, C, STOK], F32R, bb_stack)
        x_b = sb("x_b", [P, 2, GT, D], F32, bb_stack)
        x1 = sb("x1", [P, GT, D], F32, bb_stack)
        bn_s = sb("bn_s", [P, GT, 6], F32, bb_stack)
        bn_a = sb("bn_a", [P, GT, 2], F32, bb_stack)
        bn_v = sb("bn_v", [P, GT], F32, bb_stack)
        bn_i = sb("bn_i", [P, GT], I32, bb_stack)
        bn_t = sb("bn_t", [P, GT], F32, bb_stack)
        bn_r = sb("bn_r", [P, GT], F32, bb_stack)
        x1T = sb("x1T", [P, 2, 2 * D], F32, bb_stack)
        probs = sb("probs", [P, GT, E], F32, bb_stack)
        cand = sb("cand", [P, GT, E], F32, bb_stack)
        rest = sb("rest", [P, GT, E], F32, bb_stack)
        pick = sb("pick", [P, 2, GT, E], F32, bb_stack)
        chosen = sb("chosen", [P, GT, E], F32, bb_stack)
        chosen_bf = sb("chosen_bf", [P, GT + 1, E], BF16, bb_stack)
        red = sb("red", [P, GT], F32, bb_stack)
        spot = sb("spot", [P, GT, E], F32, bb_stack)
        spot_k = sb("spot_k", [P, 2, GT], F32, bb_stack)
        spot_i = sb("spot_i", [P, 2, GT, 2], I32, bb_stack)
        bb_stack.close()
        c_stack = ExitStack()
        w1_hi.append(sb("w1_hi1", [P, C, FH], F32R, c_stack))
        w1_lo.append(sb("w1_lo1", [P, C, FH], F32R, c_stack))
        w2_hi.append(sb("w2_hi1", [P, M, D], F32R, c_stack))
        w2_lo.append(sb("w2_lo1", [P, M, D], F32R, c_stack))
        xT_full = sb("xT_full", [P, C, BT], F32, c_stack)
        xT_hi = sb("xT_hi", [P, C, BT], F32R, c_stack)
        xT_lo = sb("xT_lo", [P, C, BT], F32R, c_stack)
        hid = sb("hid", [P, M, BT], F32, c_stack)
        hid_hi = sb("hid_hi", [P, M, BT], F32R, c_stack)
        hid_lo = sb("hid_lo", [P, M, BT], F32R, c_stack)
        y = sb("y", [P, BI, D], F32, c_stack)
        c_stack.close()
        b_stack.close()

        lists = nc.dram_tensor("lists", [E * CAP, ROW], F32).ap()
        h_store = nc.dram_tensor("h_store", [SBN, 2, P, C, STOK], F32).ap()

        s_c = sem("s_c")
        s_wmod = sem("s_wmod")
        s_wqk = sem("s_wqk")
        s_small = sem("s_small")
        s_fold_in = sem("s_fold_in")
        s_const = sem("s_const")
        s_cT = sem("s_cT")
        s_cTc = sem("s_cTc")
        s_silu_e = sem("s_silu_e")
        s_silu = sem("s_silu")
        s_mod = sem("s_mod")
        s_modr = sem("s_modr")
        s_bgp = sem("s_bgp")
        s_bgr = sem("s_bgr")
        s_whqk = sem("s_whqk")
        s_wlqk = sem("s_wlqk")
        s_wvT = sem("s_wvT")
        s_wvTc = sem("s_wvTc")
        s_x = sem("s_x")
        s_ln = sem("s_ln")
        s_xn = sem("s_xn")
        s_xt = sem("s_xt")
        s_hhi = sem("s_hhi")
        s_hlo = sem("s_hlo")
        s_hk = sem("s_hk")
        s_hst = sem("s_hst")
        s_kt = sem("s_kt")
        s_nm = sem("s_nm")
        s_ke = sem("s_ke")
        s_al = sem("s_al")
        s_nmo = sem("s_nmo")
        s_kT = sem("s_kT")
        s_khi = sem("s_khi")
        s_klo = sem("s_klo")
        s_ctx = sem("s_ctx")
        s_acc = sem("s_acc")
        s_q = sem("s_q")
        s_qs = sem("s_qs")
        s_qe = sem("s_qe")
        s_qr = sem("s_qr")
        s_qn = sem("s_qn")
        s_qhi = sem("s_qhi")
        s_qlo = sem("s_qlo")
        s_ctxn = sem("s_ctxn")
        s_cw = sem("s_cw")
        s_cwc = sem("s_cwc")
        s_fold = sem("s_fold")
        s_foldr = sem("s_foldr")
        s_xb = [sem(f"s_xb{i}") for i in range(2)]
        s_hb = [sem(f"s_hb{i}") for i in range(2)]
        s_at = sem("s_at")
        s_x1 = sem("s_x1")
        s_x1out = [sem(f"s_x1out{i}") for i in range(2)]
        s_row = sem("s_row")
        s_rT = sem("s_rT")
        s_rTc = sem("s_rTc")
        s_lg = sem("s_lg")
        s_lgs = sem("s_lgs")
        s_pe = sem("s_pe")
        s_ch = sem("s_ch")
        s_rk = sem("s_rk")
        s_spot = sem("s_spot")
        s_list = [sem(f"s_list{i}") for i in range(2)]
        s_counts = sem("s_counts")
        s_pad = sem("s_pad")
        s_padw = sem("s_padw")
        s_b2 = sem("s_b2")
        s_wraw = sem("s_wraw")
        s_w2g = sem("s_w2g")
        s_whi = sem("s_whi")
        s_wlo = sem("s_wlo")
        s_rows = sem("s_rows")
        s_meta = sem("s_meta")
        s_bt = sem("s_bt")
        s_bfull = sem("s_bfull")
        s_blo = sem("s_blo")
        s_f1 = sem("s_f1")
        s_gelu = sem("s_gelu")
        s_hid = sem("s_hid")
        s_f2 = sem("s_f2")
        s_y = sem("s_y")
        s_added = sem("s_added")
        s_done = sem("s_done")
        s_turn = sem("s_turn")
        s_turn_dve = sem("s_turn_dve")
        s_turn_pe = sem("s_turn_pe")
        s_turn_act = sem("s_turn_act")
        s_turn_pool = sem("s_turn_pool")
        s_dve = sem("s_dve")
        s_pool = sem("s_pool")

        TWO = 2
        FOUR = 4
        EIGHT = 8
        ONE = 1
        DMA2 = 32
        LISTED = 16 * 2 * GT
        G_END = 2 * LISTED
        CREDIT = 16

        KT, TR, CX = 4, 6, 7
        AT, RT, LG, RK = 0, 4, 6, 7
        AHEAD = 7
        XT = 5
        XTB, Y0 = 4, 5

        x_t = x.rearrange("a (t p) d -> p (a t) d", p=P)
        out_t = out[0:N, :].rearrange("(t p) d -> p t d", p=P)

        def three(pairs):
            ops = [(a, b) for (ah, al), (bh, bl) in pairs for a, b in ((ah, bh), (ah, bl), (al, bh))]
            return [(a, b, i == 0, i == len(ops) - 1) for i, (a, b) in enumerate(ops)]

        def superblocks(eng, body):
            with eng.Fori(0, SBN - 2) as s:
                body(s, True, True)
            body(SBN - 2, True, False)
            body(SBN - 1, False, False)

        def experts(eng, reg, body):
            def one(e, par, last):
                nb = eng.value_load(blocks[0:1, bass.ds(e, 1)], min_val=1, max_val=MAXB)
                body(e, par, nb, last)
            with eng.Fori(0, E // 2 - 1) as ep:
                one(ep * 2, 0, False)
                one(ep * 2 + 1, 1, False)
            one(E - 2, 0, False)
            one(E - 1, 1, True)

        def block_counter(eng, name):
            reg = eng.alloc_register(name)
            eng.reg_mov(reg, 0)
            return reg

        def now(eng, reg):
            return eng.snap(reg, min_val=0, max_val=N // BT * 2 + E)

        block = ctx.enter_context(nc.Block())

        @block.sync
        def _(sp):
            def wait_reg(s, value):
                sp.wait_ge(s, value)
                sp.sem_inc(s_turn, 1)

            for s in s_x1out:
                sp.sem_inc(s, CREDIT)
            sp.dma_start(c_rows[:, :], cvec.rearrange("a (c p) -> (a c) p", p=P)).then_inc(s_c, 16)
            sp.dma_start(b1_rows[:, :], b1.rearrange("e (m p) -> (e m) p", p=P)).then_inc(s_c, 16)
            sp.dma_start(x_in[:, :, :], x_t[:, 0:ST, :]).then_inc(s_x, 16)
            sp.dma_start(wmod_sb[:, :, :], wmod.rearrange("(c p) n -> p c n", p=P)).then_inc(s_wmod, 16)
            sp.dma_start(wqk_raw[:, :, :], w_qkv[:, 0:2 * HD].rearrange("(c p) n -> p c n", p=P)).then_inc(s_wqk, 16)
            sp.dma_start(bo_bc[:, :], b_out.partition_broadcast(P)).then_inc(s_small, 16)
            sp.dma_start(bg_bc[:, :], bg.partition_broadcast(P)).then_inc(s_small, 16)
            sp.dma_start(wg_raw[:, :, :], Wg.rearrange("(c p) e -> p c e", p=P)).then_inc(s_small, 16)
            sp.dma_start(wv_raw[:, :, :], w_qkv[:, 2 * HD:3 * HD].rearrange("(c p) n -> p c n", p=P)).then_inc(s_fold_in, 16)
            sp.dma_start(wout_sb[:, :, :], w_out.rearrange("(j p) n -> p j n", p=P)).then_inc(s_fold_in, 16)

            def spread(s, load_next, reuse):
                if load_next:
                    wait_reg(s_xn, s + 1)
                    sp.dma_start(x_in[:, :, :], x_t[:, bass.ds((s + 1) * ST, ST), :]).then_inc(s_x, 16)
                if reuse:
                    wait_reg(s_kt, (s - 1) * J)
                wait_reg(s_hlo, (s + 1) * C)
                par = s & 1
                sp.dma_start(h_k[:, bass.ds(par, 1), :, :, :].rearrange("p a b c t -> p (a b c t)").bitcast(F32),
                             h_q[:, :, :, :].rearrange("p b c t -> p (b c t)").bitcast(F32)).then_inc(s_hk, 16)
                sp.dma_start(h_store[bass.ds(s, 1), :, :, :, :].rearrange("a b p c t -> p (a b) (c t)"),
                             h_q[:, :, :, :].rearrange("p b c t -> p b (c t)").bitcast(F32)).then_inc(s_hst, 16)

            spread(0, True, False)
            spread(1, True, False)
            with sp.Fori(2, SBN - 1) as s:
                spread(s, True, True)
            spread(SBN - 1, False, True)

            sp.wait_ge(s_ctx, SBN * J + TWO)
            sp.wait_ge(s_acc, SBN * J + TWO)
            sp.wait_ge(s_qlo, TILES)
            sp.wait_ge(s_nmo, SBN * J + J)
            sp.wait_ge(s_hk, 16 * SBN)
            sp.wait_ge(s_hst, 16 * SBN)

            def load_group(g):
                par = g % 2
                if g >= 2:
                    sp.wait_ge(s_x1, (g - 1) * GT + EIGHT)
                    sp.wait_ge(s_at, (g - 1) * GT)
                for part in range(2):
                    for u in range(2):
                        sp.dma_start(h_b[:, par, part, u, :, :].rearrange("p c t -> p (c t)").bitcast(F32),
                                     h_store[2 * g + u, part, :, :, :].rearrange("p c t -> p (c t)")).then_inc(s_hb[par], 16)
                sp.dma_start(x_b[:, par, :, :], x_t[:, g * GT:(g + 1) * GT, :]).then_inc(s_xb[par], 16)

            load_group(0)
            sp.dma_start(w1_raw[:, :, :], W1[0, :, :].rearrange("(c p) n -> p c n", p=P)).then_inc(s_wraw, 16)
            sp.dma_start(w2_raw[:, :, :], W2[0, :, :].rearrange("(m p) n -> p m n", p=P)).then_inc(s_wraw, 16)
            sp.dma_start(b2_bc[:, :, :].rearrange("p e d -> p (e d)"), b2.rearrange("e d -> (e d)").partition_broadcast(P)).then_inc(s_b2, 16)
            load_group(1)
            sp.wait_ge(s_pad, 1)
            for g in range(GROUPS):
                if 1 <= g < GROUPS - 1:
                    load_group(g + 1)
                for half in range(2):
                    sp.wait_ge(s_x1, g * GT + half * 4 + 4 + EIGHT)
                    t0 = g * GT + half * 4
                    sp.dma_start(out_t[:, t0:t0 + 4, :], x1[:, half * 4:half * 4 + 4, :]).then_inc(s_x1out[half], 16)
            sp.wait_ge(s_counts, 1)
            with sp.Fori(0, E) as e:
                n = sp.value_load(counts[0:1, bass.ds(e, 1)], min_val=0, max_val=N)
                sp.dma_start(lists[bass.ds(e * CAP + n, BT), :].rearrange("(p i) c -> p i c", i=BI), pad[:, :, :]).then_inc(s_padw, 16)
            sp.wait_ge(s_padw, 16 * E)
            for par in range(2):
                sp.wait_ge(s_list[par], G_END)

            g = block_counter(sp, "g_sp")

            def load_rows(e, b):
                gv = now(sp, g)
                wait_reg(s_meta, gv + ONE)
                wait_reg(s_bt, gv + ONE)
                sp.dma_start(listed[:, :, :], lists[bass.ds(e * CAP + b * BT, BT), :].rearrange("(p i) c -> p i c", i=BI)).then_inc(s_rows, 16)
                sp.reg_add(g, g, 1)

            def expert(e, par, nb, last):
                load_rows(e, 0)
                if not last:
                    wait_reg(s_wlo, e + 1)
                    sp.dma_start(w1_raw[:, :, :], W1[bass.ds(e + 1, 1), :, :].rearrange("a (c p) n -> p (a c) n", p=P)).then_inc(s_wraw, 16)
                    sp.dma_start(w2_raw[:, :, :], W2[bass.ds(e + 1, 1), :, :].rearrange("a (m p) n -> p (a m) n", p=P)).then_inc(s_wraw, 16)
                with sp.Fori(1, nb) as b:
                    load_rows(e, b)

            experts(sp, g, expert)
            load_rows(0, 0)
            sp.wait_ge(s_done, 1)
            for half in range(2):
                sp.wait_ge(s_x1out[half], 16 * GROUPS + CREDIT)

        @block.gpsimd
        def _(pool):
            pool.memset(ident[:, :], 0.0).then_inc(s_pool, 1)
            pool.memset(before_bf[:, :], 1.0).then_inc(s_pool, 1)
            pool.wait_ge(s_pool, 2)
            pool.affine_select(out=ident[:, :], in_=ident[:, :], compare_op=ALU.not_equal, fill=1.0,
                               base=0, pattern=[[-1, P]], channel_multiplier=1).then_inc(s_const, 1)
            pool.affine_select(out=before_bf[:, :], in_=before_bf[:, :], compare_op=ALU.is_gt, fill=0.0,
                               base=0, pattern=[[1, P]], channel_multiplier=-1).then_inc(s_const, 1)
            pool.memset(ones_bf[:, :], 1.0).then_inc(s_const, 1)
            pool.memset(ones_row[:, :], 1.0).then_inc(s_const, 1)
            pool.iota(lane[:, :], pattern=[[-1, E]], base=E, channel_multiplier=0,
                      allow_small_or_imprecise_dtypes=True).then_inc(s_const, 1)
            pool.iota(list_start[:, :], pattern=[[CAP, E]], base=0, channel_multiplier=0,
                      allow_small_or_imprecise_dtypes=True).then_inc(s_const, 1)
            pool.iota(list_next[:, :], pattern=[[CAP, E]], base=0, channel_multiplier=0,
                      allow_small_or_imprecise_dtypes=True).then_inc(s_const, 1)
            pool.iota(token_of[:, :], pattern=[[P, GT]], base=0, channel_multiplier=1,
                      allow_small_or_imprecise_dtypes=True).then_inc(s_const, 1)
            pool.iota(pad_id[:, :], pattern=[[1, BI]], base=N, channel_multiplier=BI).then_inc(s_const, 1)

            def h_lo(s, c):
                pool.wait_ge(s_hhi, s * C + (c + 1))
                pool.tensor_tensor(h_q[:, 1, c, :], h_full[:, c, :], h_q[:, 0, c, :].bitcast(F32), ALU.subtract).then_inc(s_hlo, 1)

            def q_parts(s, first, last):
                for i in range(first, last):
                    pool.wait_ge(s_qr, s * ST + (i + 1))
                    qe = q_exp[:, i % 2, :].rearrange("p (h d) -> p h d", d=DH)
                    pool.tensor_tensor(qe, qe, bc(q_rec[:, i % 2, :], 2, [P, 2 * J, DH]), ALU.mult).then_inc(s_qn, 1)
                    pool.wait_ge(s_qhi, s * ST + (i + 1))
                    qh = q_hl[:, bass.ds(s & 1, 1), i, :, :, :].rearrange("p a j l d -> p (a j) l d")
                    pool.tensor_tensor(qh[:, :, 1, :], q_exp[:, i % 2, :].rearrange("p (j d) -> p j d", d=P),
                                       qh[:, :, 0, :].bitcast(F32), ALU.subtract).then_inc(s_qlo, 1)

            pool.wait_ge(s_whqk, 1)
            pool.tensor_tensor(wqk_lo[:, :, 0:HD], wqk_raw[:, :, 0:HD], wqk_hi[:, :, 0:HD].bitcast(F32), ALU.subtract).then_inc(s_wlqk, 1)

            for c in range(C):
                h_lo(0, c)
            q_parts(0, 0, 2)
            for c in range(C):
                h_lo(1, c)
            q_parts(0, 2, ST)
            with pool.Fori(1, SBN - 1) as s:
                q_parts(s, 0, 2)
                for c in range(C):
                    h_lo(s + 1, c)
                q_parts(s, 2, ST)
            q_parts(SBN - 1, 0, ST)

            def w_times_gb():
                pool.tensor_tensor(w2_raw[:, :, :], w2_raw[:, :, :], bc(gates[:, 1, :], 1, [P, M, D]), ALU.mult).then_inc(s_w2g, 1)

            def w1_low(e, par):
                pool.wait_ge(s_whi, e * 2 + 1)
                pool.tensor_tensor(w1_lo[par][:, :, :], w1_raw[:, :, :], w1_hi[par][:, :, :].bitcast(F32), ALU.subtract)

            def w2_low(e, par):
                pool.wait_ge(s_whi, e * 2 + 2)
                pool.tensor_tensor(w2_lo[par][:, :, :], w2_raw[:, :, :], w2_hi[par][:, :, :].bitcast(F32), ALU.subtract).then_inc(s_wlo, 1)

            pool.wait_ge(s_b2, 16)
            pool.tensor_tensor(b2_bc[:, :, :], b2_bc[:, :, :], bc(gates[:, 1, :], 1, [P, E, D]), ALU.mult)
            pool.wait_ge(s_wraw, 32)
            w_times_gb()
            w1_low(0, 0)
            w2_low(0, 0)

            for g in range(GROUPS):
                pool.wait_ge(s_spot, g + 1 + TWO)
                for i in range(GT):
                    for k in range(2):
                        pool.indirect_dma_start(lists[:, :], bass.IndirectOffsetOnAxis(ap=spot_i[:, g % 2, i, k:k + 1], axis=0),
                                                rows[:, g % RB, i, :], None).then_inc(s_list[g % 2], 16)

            for half in range(2):
                pool.wait_ge(s_x1out[half], 16 * GROUPS + CREDIT)
            pool.wait_ge(s_counts, 1)
            for i in range(BI):
                pool.dma_start(out[N + i * P:N + (i + 1) * P, :], pad[:, i, 0:D]).then_inc(s_added, 16)
            g = block_counter(pool, "g_pool")

            def expert(e, par, nb, last):
                def add_rows(gv, i):
                    pool.wait_ge(s_y, gv * 2 + (i + 1 + TWO))
                    pool.wait_ge(s_added, gv * 32 + (16 * i + DMA2))
                    pool.sem_inc(s_turn_pool, 1)
                    pool.indirect_dma_start(out[:, :], bass.IndirectOffsetOnAxis(ap=y_id[:, i:i + 1], axis=0),
                                            y[:, i, :], None, compute_op=ALU.add).then_inc(s_added, 16)

                gv = now(pool, g)
                if not last:
                    pool.wait_ge(s_wraw, e * 32 + 64)
                    w_times_gb()
                add_rows(gv, 0)
                if not last:
                    w1_low(e + 1, 1 - par)
                add_rows(gv, 1)
                if not last:
                    w2_low(e + 1, 1 - par)
                pool.reg_add(g, g, 1)
                with pool.Fori(1, nb) as b:
                    gv = now(pool, g)
                    for i in range(BI):
                        add_rows(gv, i)
                    pool.reg_add(g, g, 1)

            experts(pool, g, expert)
            pool.wait_ge(s_added, now(pool, g) * 32 + DMA2)
            pool.sem_inc(s_done, 1)

        @block.scalar
        def _(act):
            act.sem_inc(s_ke, TWO)
            act.sem_inc(s_nmo, J)
            act.sem_inc(s_rTc, TWO)
            act.sem_inc(s_gelu, FOUR)

            def h_hi(s, c, buffers_used):
                act.wait_ge(s_xt, s * C + (c + 1))
                if buffers_used and c == 0:
                    act.wait_ge(s_q, s * ST)
                    act.wait_ge(s_hk, s * 16)
                    act.wait_ge(s_hst, s * 16)
                act.activation(h_q[:, 0, c, :], ps[:, c, :], ACT.Identity, bias=modc[:, 0, c:c + 1],
                               scale=modc[:, 1, c:c + 1])
                if buffers_used:
                    act.wait_ge(s_hlo, s * C + (c - 1))
                act.activation(h_full[:, c, :], ps[:, c, :], ACT.Identity, bias=modc[:, 0, c:c + 1],
                               scale=modc[:, 1, c:c + 1]).then_inc(s_hhi, 1)

            def norm_x(s, reuse, tiles=range(ST)):
                if 0 in tiles:
                    act.wait_ge(s_ln, s + 1)
                    if reuse:
                        act.wait_ge(s_xt, s * C)
                for t in tiles:
                    last = act.activation(xn[:, t, :], x_in[:, t, :], ACT.Identity, bias=ln_b[:, t:t + 1], scale=ln_r[:, t:t + 1])
                if ST - 1 in tiles:
                    last.then_inc(s_xn, 1)

            def q_e(s, i):
                act.wait_ge(s_qs, s * ST + (i + 1))
                act.activation(q_exp[:, i % 2, :], q_exp[:, i % 2, :], ACT.Exp, scale=SCALE).then_inc(s_qe, 1)

            def q_hi(s, i):
                act.wait_ge(s_qn, s * ST + (i + 1))
                qh = q_hl[:, bass.ds(s & 1, 1), i, :, :, :].rearrange("p a j l d -> p (a j) l d")
                act.activation(qh[:, :, 0, :], q_exp[:, i % 2, :].rearrange("p (j d) -> p j d", d=P), ACT.Copy).then_inc(s_qhi, 1)

            act.wait_ge(s_cTc, 1)
            act.activation(silu_t[:, :], silu_c[:, :], ACT.Exp, scale=-1.0).then_inc(s_silu_e, 1)
            norm_x(0, False)
            act.wait_ge(s_modr, 1)
            for c in range(C):
                h_hi(0, c, False)
            act.wait_ge(s_wqk, 16)
            q_e(0, 0)
            norm_x(1, True)
            q_e(0, 1)
            q_hi(0, 0)
            q_e(0, 2)
            q_hi(0, 1)
            q_e(0, 3)
            for c in range(C):
                h_hi(1, c, True)
            q_hi(0, 2)

            def body(s, more, more2):
                def k_e(j):
                    act.wait_ge(s_nm, s * J + (j + 1))
                    act.wait_ge(s_kT, s * J + (j - 1 + TWO))
                    act.activation(k_exp[:, j % 2, :], ps[:, KT + j % 2, :], ACT.Exp, bias=k_new[:, j:j + 1],
                                   accum_out=k_part[:, j:j + 1]).then_inc(s_ke, 1)
                    act.activation(k_alpha[:, j:j + 1], k_nmax[:, j:j + 1], ACT.Exp, scale=-1.0, bias=k_new[:, j:j + 1]).then_inc(s_al, 1)

                def k_h(j):
                    act.wait_ge(s_kT, s * J + (j + 1 + TWO))
                    act.wait_ge(s_ctx, s * J + (j - 1 + TWO))
                    act.activation(k_hi[:, j % 2, :, :].rearrange("p t e -> p (t e)"), ps[:, TR, :], ACT.Copy).then_inc(s_khi, 1)
                    act.wait_ge(s_al, s * J + (j + 1))
                    act.activation(k_nmax[:, j:j + 1], k_new[:, j:j + 1], ACT.Copy).then_inc(s_nmo, 1)

                for j in range(J):
                    if j >= 1:
                        k_h(j - 1)
                    k_e(j)
                    if j == 0:
                        q_hi(s, 3)
                    if more:
                        if j == 2:
                            act.wait_ge(s_ctx, s * J + TWO)
                        for slot, step, i in ((1, q_e, 0), (2, q_e, 1), (3, q_hi, 0), (4, q_hi, 1),
                                              (5, q_e, 2), (6, q_e, 3), (7, q_hi, 2)):
                            if j == slot:
                                step(s + 1, i)
                    if more2 and j in (XT - 2, XT - 1):
                        half = (j - XT + 2) * 2
                        norm_x(s + 2, True, range(half, half + 2))
                    if more2 and XT <= j < XT + C:
                        h_hi(s + 2, j - XT, True)
                k_h(J - 1)

            superblocks(act, body)

            for b in range(4):
                act.wait_ge(s_cw, b + 1)
                act.activation(cw[:, 2 * b:2 * b + 2, :].rearrange("p j d -> p (j d)"), ps[:, b, :], ACT.Copy).then_inc(s_cwc, 1)

            def w1_part(e, par):
                act.activation(w1_hi[par][:, :, :], w1_raw[:, :, :], ACT.Copy).then_inc(s_whi, 1)

            def w2_part(e, par):
                act.wait_ge(s_w2g, e + 1)
                act.activation(w2_hi[par][:, :, :], w2_raw[:, :, :], ACT.Copy).then_inc(s_whi, 1)

            act.wait_ge(s_wraw, 32)
            w1_part(0, 0)
            w2_part(0, 0)

            with act.Fori(0, GROUPS // 2) as gg:
                for par in range(2):
                    for n in range(GT // 2):
                        done = par * GT // 2 + n
                        act.wait_ge(s_rT, gg * GT + (done + 1))
                        act.wait_ge(s_lg, gg * GT + (done - 1 + TWO))
                        act.activation(x1T[:, n % 2, :], ps[:, RT + n % 2, :], ACT.Copy).then_inc(s_rTc, 1)
                    act.wait_ge(s_lgs, gg * 2 + (par + 1 + TWO))
                    act.activation(probs[:, :, :], probs[:, :, :], ACT.Exp).then_inc(s_pe, 1)

            act.wait_ge(s_counts, 1)
            g = block_counter(act, "g_act")

            def block_full(n):
                act.wait_ge(s_bt, n + 1 + ONE)
                if not isinstance(n, int):
                    act.wait_ge(s_blo, n)
                    act.sem_inc(s_turn_act, 1)
                for c in range(C):
                    act.activation(xT_full[:, c, :], ps[:, XTB, c * BT:(c + 1) * BT], ACT.Identity,
                                   bias=modc[:, 2, c:c + 1], scale=modc[:, 3, c:c + 1]).then_inc(s_bfull, 1)

            for par in range(2):
                act.wait_ge(s_list[par], G_END)
                act.wait_ge(s_x1out[par], 16 * GROUPS + CREDIT)
            block_full(0)

            def expert(e, par, nb, last):
                def rows_block(prepare):
                    gv = now(act, g)
                    for k in range(M // 2):
                        act.wait_ge(s_f1, gv * 4 + (k + 1))
                        act.wait_ge(s_hid, gv * 4 + (k + 1))
                        act.sem_inc(s_turn_act, 1)
                        for m in (2 * k, 2 * k + 1):
                            ins = act.activation(hid[:, m, :], ps[:, k, (m % 2) * BT:(m % 2 + 1) * BT], ACT.Gelu_apprx_tanh,
                                                 bias=b1_col[:, bass.ds(e, 1), m])
                        ins.then_inc(s_gelu, 1)
                        if prepare and k == M // 2 - 1:
                            act.wait_ge(s_f2, gv * 2 + TWO)
                            act.sem_inc(s_turn_act, 1)
                            act.wait_ge(s_wraw, e * 32 + 64)
                            act.sem_inc(s_turn_act, 1)
                            w1_part(e + 1, 1 - par)
                    block_full(gv + 1)
                    if prepare:
                        w2_part(e + 1, 1 - par)
                    act.reg_add(g, g, 1)

                rows_block(not last)
                with act.Fori(1, nb) as b:
                    rows_block(False)

            experts(act, g, expert)

        @block.vector
        def _(dve):
            chain = Link(dve, s_dve)
            link = chain.link
            for s in (s_klo, s_acc, s_lgs, s_spot, s_y):
                dve.sem_inc(s, TWO)
            dve.sem_inc(s_hid, FOUR)
            dve.sem_inc(s_x1, EIGHT)
            dve.sem_inc(s_meta, ONE)

            def inverse_root(r, v, i, t):
                link(dve.tensor_scalar(i, v.bitcast(I32), 1, None, ALU.logical_shift_right))
                link(dve.tensor_scalar(r.bitcast(I32), i, -1.0, float(0x5f3759df), ALU.mult, ALU.add))
                for _ in range(3):
                    link(dve.tensor_tensor(t, r, r, ALU.mult))
                    link(dve.scalar_tensor_tensor(t, t, -0.5, v, ALU.mult, ALU.mult))
                    link(dve.scalar_tensor_tensor(r, t, 1.5, r, ALU.add, ALU.mult))

            def variance(s):
                dve.wait_ge(s_x, s * 16 + 16)
                for t in range(ST):
                    last = dve.bn_stats(ln_s[:, t, :], x_in[:, t, :])
                chain.link_apart(last, s_turn_dve)
                if not (isinstance(s, int) and s == 0):
                    dve.wait_ge(s_xn, s)
                    dve.sem_inc(s_turn_dve, 1)
                for t in range(ST):
                    last = dve.bn_aggr(ln_a[:, t, :], ln_s[:, t, :])
                link(last)
                link(dve.tensor_scalar(ln_v[:, :], ln_a[:, :, 1], EPS, None, ALU.add))

            def deviation(s):
                inverse_root(ln_r[:, :], ln_v[:, :], ln_i[:, :], ln_t[:, :])
                dve.scalar_tensor_tensor(ln_b[:, :], ln_a[:, :, 0], -1.0, ln_r[:, :], ALU.mult, ALU.mult).then_inc(s_ln, 1)

            def q_a(s, i, reuse):
                dve.wait_ge(s_q, s * ST + (i + 1))
                if reuse:
                    dve.wait_ge(s_qlo, s * ST + (i - 1))
                b = (i % 2) * 2
                q = ps[:, b:b + 2, :].rearrange("p b (h d) -> p (b h) d", d=DH)
                link(dve.tensor_reduce(q_max[:, i % 2, :], q, AX, ALU.max))
                dve.tensor_tensor(q_exp[:, i % 2, :].rearrange("p (h d) -> p h d", d=DH), q,
                                  bc(q_max[:, i % 2, :], 2, [P, 2 * J, DH]), ALU.subtract).then_inc(s_qs, 1)

            def q_b(s, i):
                dve.wait_ge(s_qe, s * ST + (i + 1))
                link(dve.tensor_reduce(q_sum[:, i % 2, :], q_exp[:, i % 2, :].rearrange("p (h d) -> p h d", d=DH), AX, ALU.add))
                dve.reciprocal(q_rec[:, i % 2, :], q_sum[:, i % 2, :]).then_inc(s_qr, 1)

            variance(0)
            deviation(0)
            dve.wait_ge(s_cT, 1)
            dve.tensor_copy(b1_col[:, :, :].rearrange("p e m -> p (e m)"), ps[:, 0, 64:128])
            dve.tensor_copy(silu_c[:, :], ps[:, 0, 0:C]).then_inc(s_cTc, 1)
            dve.wait_ge(s_silu_e, 1)
            link(dve.tensor_scalar(silu_t[:, :], silu_t[:, :], 1.0, None, ALU.add))
            link(dve.reciprocal(silu_t[:, :], silu_t[:, :]))
            link(dve.tensor_tensor(silu_c[:, :], silu_c[:, :], silu_t[:, :], ALU.mult))
            dve.tensor_copy(silu_b[:, :, :], bc(silu_c[:, :], 2, [P, C, P])).then_inc(s_silu, 1)
            dve.memset(ctx_acc[:, :, :], 0.0)
            dve.memset(k_sum[:, :], 0.0)
            link(dve.memset(k_nmax[:, :], BIG))
            dve.wait_ge(s_mod, 1)
            link(dve.tensor_copy(modc[:, :, :].rearrange("p k c -> p (k c)"), ps[:, 1, 0:4 * C]))
            link(dve.tensor_scalar(modc[:, 1, :], modc[:, 1, :], 1.0, None, ALU.add))
            link(dve.tensor_scalar(modc[:, 3, :], modc[:, 3, :], 1.0, None, ALU.add))
            dve.tensor_copy(shift_b[:, :, :], bc(modc[:, 2, :], 2, [P, C, P])).then_inc(s_modr, 1)
            g2 = ps[:, 2, :].rearrange("p (k d) -> p k d", d=D)
            dve.tensor_scalar(gate_s[:, :, :], g2, 0.0, 2.0, ALU.is_ge, ALU.mult)
            link(dve.tensor_scalar(gate_m[:, :, :], g2, -1.0, None, ALU.mult))
            link(dve.tensor_tensor(gate_m[:, :, :], gate_m[:, :, :], g2, ALU.max))
            link(dve.tensor_scalar(gate_m[:, :, :], gate_m[:, :, :], 0.25, None, ALU.max))
            link(dve.scalar_tensor_tensor(gates[:, :, :], gate_s[:, :, :], 1.0, gate_m[:, :, :], ALU.subtract, ALU.mult))
            dve.wait_ge(s_wqk, 16)
            dve.tensor_copy(wqk_hi[:, :, 0:HD], wqk_raw[:, :, 0:HD]).then_inc(s_whqk, 1)
            dve.tensor_copy(wqk_hi[:, :, HD:2 * HD], wqk_raw[:, :, HD:2 * HD]).then_inc(s_whqk, 1)
            dve.wait_ge(s_whqk, 2)
            dve.tensor_tensor(wqk_lo[:, :, HD:2 * HD], wqk_raw[:, :, HD:2 * HD], wqk_hi[:, :, HD:2 * HD].bitcast(F32), ALU.subtract).then_inc(s_wlqk, 1)
            dve.wait_ge(s_small, 48)
            link(dve.tensor_tensor(bo_bc[:, :], bo_bc[:, :], gates[:, 0, :], ALU.mult))
            dve.tensor_tensor(wg_mod[:, :, :], wg_raw[:, :, :], bc(modc[:, 3, :], 2, [P, C, E]), ALU.mult)
            dve.wait_ge(s_bgp, 1)
            dve.tensor_tensor(bg_bc[:, :], bg_bc[:, :], ps[:, 3, 0:E], ALU.add).then_inc(s_bgr, 1)
            for half in range(2):
                dve.wait_ge(s_wvT, half + 1)
                dve.tensor_copy(wvT[:, 4 * half:4 * half + 4, :], ps[:, 4 + 2 * half:6 + 2 * half, :].rearrange("p b (j f) -> p (b j) f", f=D)).then_inc(s_wvTc, 1)

            variance(1)
            q_a(0, 0, False)
            deviation(1)
            q_a(0, 1, False)
            q_b(0, 0)
            q_a(0, 2, True)
            q_b(0, 1)
            q_a(0, 3, True)
            q_b(0, 2)
            q_b(0, 3)
            dve.wait_ge(s_wlqk, 2)
            dreg = dve.alloc_register("dve_chain")
            chain.enter(dreg)

            def body(s, more, more2):
                def k_m(j):
                    dve.wait_ge(s_nmo, s * J + j + 1)
                    dve.wait_ge(s_kt, s * J + (j + 1))
                    link(dve.tensor_reduce(k_blk[:, j:j + 1], ps[:, KT + j % 2, :], AX, ALU.max, negate=True))
                    dve.tensor_tensor(k_new[:, j:j + 1], k_nmax[:, j:j + 1], k_blk[:, j:j + 1], ALU.min).then_inc(s_nm, 1)

                def k_l(j):
                    dve.wait_ge(s_khi, s * J + (j + 1))
                    dve.tensor_tensor(k_lo[:, j % 2, :, :].rearrange("p t e -> p (t e)"), ps[:, TR, :],
                                      k_hi[:, j % 2, :, :].rearrange("p t e -> p (t e)").bitcast(F32), ALU.subtract).then_inc(s_klo, 1)

                def acc(j):
                    dve.wait_ge(s_ctx, s * J + (j + 1 + TWO))
                    dve.wait_ge(s_al, s * J + (j + 1))
                    dve.wait_ge(s_acc, s * J + (j + TWO))
                    al = k_alpha[:, j:j + 1]
                    dve.scalar_tensor_tensor(k_sum[:, j:j + 1], k_sum[:, j:j + 1], al, k_part[:, j:j + 1], ALU.mult, ALU.add)
                    dve.scalar_tensor_tensor(ctx_acc[:, j, :], ctx_acc[:, j, :], al, ps[:, CX, 0:2 * P], ALU.mult, ALU.add).then_inc(s_acc, 1)

                for j in range(J):
                    k_m(j)
                    if j >= 1:
                        k_l(j - 1)
                    if j >= 2:
                        acc(j - 2)
                    if more:
                        for slot, step in ((0, lambda: q_a(s + 1, 0, True)), (1, lambda: q_a(s + 1, 1, True)),
                                           (2, lambda: q_b(s + 1, 0)), (3, lambda: q_b(s + 1, 1)),
                                           (4, lambda: q_a(s + 1, 2, True)), (5, lambda: q_a(s + 1, 3, True)),
                                           (6, lambda: q_b(s + 1, 2)), (7, lambda: q_b(s + 1, 3))):
                            if j == slot:
                                step()
                    if more2:
                        if j == 2:
                            variance(s + 2)
                        if j == 3:
                            deviation(s + 2)
                k_l(J - 1)
                acc(J - 2)
                acc(J - 1)
                if not isinstance(s, int) or more:
                    chain.end()
                    chain.begin()

            with dve.Fori(0, SBN - 2) as s:
                chain.begin()
                body(s, True, True)
            chain.begin()
            body(SBN - 2, True, False)
            body(SBN - 1, False, False)

            dve.wait_ge(s_acc, SBN * J + TWO)
            dve.wait_ge(s_khi, SBN * J)
            dve.wait_ge(s_qlo, TILES)
            dve.wait_ge(s_hk, 16 * SBN)
            dve.wait_ge(s_hst, 16 * SBN)
            dve.memset(ctx_n[:, :, :], 0.0)
            link(dve.reciprocal(k_rec[:, :], k_sum[:, :]))
            link(dve.tensor_tensor(ctx_acc[:, :, 0:P], ctx_acc[:, :, 0:P], ctx_acc[:, :, P:2 * P], ALU.add))
            for h in range(2):
                r = slice(h * DH, (h + 1) * DH)
                last = dve.tensor_tensor(ctx_n[r, :, r], ctx_acc[r, :, r], bc(k_rec[r, :], 2, [DH, J, DH]), ALU.mult)
            last.then_inc(s_ctxn, 1)
            dve.memset(chosen_bf[:, GT:GT + 1, :], 0.0)
            link(dve.memset(pad[:, :, :], 0.0))
            dve.wait_ge(s_const, 9)
            dve.tensor_copy(pad[:, :, ROW - 1].bitcast(I32), pad_id[:, :]).then_inc(s_pad, 1)
            dve.wait_ge(s_fold, 1)
            dve.tensor_copy(ones_r[:, :], ones_row[:, :])
            for r in range(2):
                last = dve.tensor_copy(bo_hl[0:1, 0, r, :], bo_bc[0:1, :])
            link(last)
            for r in range(2):
                dve.tensor_tensor(bo_hl[0:1, 1, r, :], bo_bc[0:1, :], bo_hl[0:1, 0, r, :].bitcast(F32), ALU.subtract)
            link(dve.tensor_tensor(fold[:, :, :], ps[:, 4:6, 0:D], bc(gates[:, 0, :], 1, [P, C, D]), ALU.mult))
            link(dve.tensor_copy(fold_hi[:, :, :], fold[:, :, :]))
            dve.tensor_tensor(fold_lo[:, :, :], fold[:, :, :], fold_hi[:, :, :].bitcast(F32), ALU.subtract).then_inc(s_foldr, 1)

            def x1_of(g):
                par, t0 = g % 2, g * GT
                dve.wait_ge(s_xb[par], g // 2 * 16 + 16)
                if g:
                    dve.wait_ge(s_row, t0)
                for n in range(GT // 2):
                    two = slice(2 * n, 2 * n + 2)
                    if n % 2 == 0:
                        dve.wait_ge(s_x1out[n // 2], g * 16 + CREDIT)
                    dve.wait_ge(s_at, t0 + (2 * n + 2))
                    dve.tensor_tensor(x1[:, two, :], ps[:, AT + n % 4, :].rearrange("p (i d) -> p i d", d=D),
                                      x_b[:, par, two, :], ALU.add).then_inc(s_x1, 2)
                    if n:
                        dve.wait_ge(s_x1, t0 + (2 * n + EIGHT))
                        for i in (2 * n - 2, 2 * n - 1):
                            dve.bn_stats(bn_s[:, i, :], x1[:, i, :])
                dve.wait_ge(s_x1, t0 + (GT + EIGHT))
                for i in (GT - 2, GT - 1):
                    last = dve.bn_stats(bn_s[:, i, :], x1[:, i, :])
                chain.link_apart(last, s_turn_dve)
                for i in range(GT):
                    last = dve.bn_aggr(bn_a[:, i, :], bn_s[:, i, :])
                link(last)
                link(dve.tensor_scalar(bn_v[:, :], bn_a[:, :, 1], EPS, None, ALU.add))
                inverse_root(bn_r[:, :], bn_v[:, :], bn_i[:, :], bn_t[:, :])

            def rows_of(g):
                if g >= RB:
                    dve.wait_ge(s_list[(g - RB) % 2], ((g - RB) // 2 + 1) * LISTED)
                for i in range(GT):
                    dve.tensor_scalar(rows[:, g % RB, i, 0:D], x1[:, i, :], bn_a[:, i, 0:1], bn_r[:, i:i + 1], ALU.subtract, ALU.mult).then_inc(s_row, 1)

            def route(g):
                shape, par = [P, GT, E], g % 2
                dve.wait_ge(s_lg, (g + 1) * GT // 2 + TWO)
                link(dve.tensor_tensor(probs[:, :, :], ps[:, LG, 0:GT * E].rearrange("p (t e) -> p t e", e=E),
                                       bc(bg_bc[:, :], 1, shape), ALU.add))
                link(dve.tensor_reduce(red[:, :], probs[:, :, :], AX, ALU.max))
                dve.tensor_tensor(probs[:, :, :], probs[:, :, :], bc(red[:, :], 2, shape), ALU.subtract).then_inc(s_lgs, 1)
                dve.wait_ge(s_pe, g + 1)
                link(dve.tensor_reduce(red[:, :], probs[:, :, :], AX, ALU.add))
                link(dve.reciprocal(red[:, :], red[:, :]))
                link(dve.tensor_tensor(probs[:, :, :], probs[:, :, :], bc(red[:, :], 2, shape), ALU.mult))
                for k, p in ((0, probs), (1, rest)):
                    link(dve.tensor_reduce(red[:, :], p[:, :, :], AX, ALU.max))
                    link(dve.tensor_tensor(cand[:, :, :], p[:, :, :], bc(red[:, :], 2, shape), ALU.is_equal))
                    link(dve.tensor_tensor(cand[:, :, :], cand[:, :, :], bc(lane[:, :], 1, shape), ALU.mult))
                    link(dve.tensor_reduce(red[:, :], cand[:, :, :], AX, ALU.max))
                    link(dve.tensor_tensor(pick[:, k, :, :], cand[:, :, :], bc(red[:, :], 2, shape), ALU.is_equal))
                    if k == 0:
                        link(dve.scalar_tensor_tensor(rest[:, :, :], pick[:, 0, :, :], -4.0, probs[:, :, :], ALU.mult, ALU.add))
                link(dve.tensor_tensor(chosen[:, :, :], pick[:, 0, :, :], pick[:, 1, :, :], ALU.add))
                dve.tensor_copy(chosen_bf[:, 0:GT, :], chosen[:, :, :]).then_inc(s_ch, 1)
                dve.wait_ge(s_ch, g + 1)
                link(dve.tensor_tensor(chosen[:, :, :], probs[:, :, :], chosen[:, :, :], ALU.mult))
                link(dve.tensor_reduce(red[:, :], chosen[:, :, :], AX, ALU.add))
                link(dve.tensor_scalar(red[:, :], red[:, :], 1e-8, None, ALU.add))
                link(dve.reciprocal(red[:, :], red[:, :]))
                dve.tensor_tensor(rows[:, g % RB, :, D:D + E], chosen[:, :, :], bc(red[:, :], 2, shape), ALU.mult)
                link(dve.tensor_copy(rows[:, g % RB, :, ROW - 1].bitcast(I32), token_of[:, :]))
                link(dve.tensor_scalar(token_of[:, :], token_of[:, :], float(GT * P), None, ALU.add))
                dve.wait_ge(s_rk, g + 1)
                link(dve.tensor_tensor(spot[:, :, :], ps[:, RK, 0:GT * E].rearrange("p (t e) -> p t e", e=E),
                                       bc(list_next[:, :], 1, shape), ALU.add))
                link(dve.tensor_tensor(list_next[:, :], list_next[:, :], ps[:, RK, GT * E:(GT + 1) * E], ALU.add))
                for k in range(2):
                    link(dve.tensor_tensor(cand[:, :, :], spot[:, :, :], pick[:, k, :, :], ALU.mult))
                    link(dve.tensor_reduce(spot_k[:, k, :], cand[:, :, :], AX, ALU.add))
                if g >= 2:
                    dve.wait_ge(s_list[par], g // 2 * LISTED)
                dve.tensor_copy(spot_i[:, par, :, :].rearrange("p t k -> p k t"), spot_k[:, :, :]).then_inc(s_spot, 1)

            x1_of(0)
            rows_of(0)
            for g in range(GROUPS):
                if g + 1 < GROUPS:
                    x1_of(g + 1)
                    rows_of(g + 1)
                route(g)

            link(dve.tensor_tensor(counts_f[:, :], list_next[:, :], list_start[:, :], ALU.subtract))
            link(dve.tensor_copy(counts[:, :], counts_f[:, :]))
            link(dve.tensor_scalar(counts_f[:, :], counts_f[:, :], float(BT - 1), None, ALU.add))
            link(dve.tensor_copy(blocks[:, :], counts_f[:, :]))
            link(dve.tensor_scalar(blocks[:, :], blocks[:, :], BT.bit_length() - 1, None, ALU.arith_shift_right))
            link(dve.tensor_scalar(blocks[:, :], blocks[:, :], 1, None, ALU.max))
            dve.sem_inc(s_counts, 1)
            dve.wait_ge(s_w2g, 1)

            g = block_counter(dve, "g_dve")
            for par in range(2):
                dve.wait_ge(s_list[par], G_END)
                dve.wait_ge(s_x1out[par], 16 * GROUPS + CREDIT)

            def block_parts(n):
                for c in range(C):
                    dve.wait_ge(s_bfull, n * C + (c + 1))
                    link(dve.tensor_copy(xT_hi[:, c, :], xT_full[:, c, :]))
                    last = dve.tensor_tensor(xT_lo[:, c, :], xT_full[:, c, :], xT_hi[:, c, :].bitcast(F32), ALU.subtract)
                last.then_inc(s_blo, 1)

            block_parts(0)
            chain.end()

            def expert(e, par, nb, last_expert):
                with dve.Fori(0, nb) as b:
                    chain.begin()
                    gv = now(dve, g)
                    for k in range(M // 2):
                        dve.wait_ge(s_gelu, gv * 4 + (k + 1 + FOUR))
                        if k == 0:
                            dve.wait_ge(s_f2, gv * 2 + TWO)
                        m = slice(2 * k, 2 * k + 2)
                        link(dve.tensor_copy(hid_hi[:, m, :], hid[:, m, :]))
                        dve.tensor_tensor(hid_lo[:, m, :], hid[:, m, :], hid_hi[:, m, :].bitcast(F32), ALU.subtract).then_inc(s_hid, 1)
                        if k == 0:
                            dve.wait_ge(s_rows, gv * 16 + 16)
                            dve.tensor_copy(listed_w[:, :, :], listed[:, :, D:D + E])
                            link(dve.tensor_copy(listed_id[:, :], listed[:, :, ROW - 1].bitcast(I32)))
                            dve.sem_inc(s_meta, 1)

                    block_parts(gv + 1)
                    dve.wait_ge(s_added, gv * 32 + DMA2)
                    dve.tensor_copy(y_w[:, :, :], listed_w[:, :, :])
                    link(dve.tensor_copy(y_id[:, :], listed_id[:, :]))

                    def rows_out(i):
                        dve.wait_ge(s_f2, gv * 2 + (i + 1 + TWO))
                        link(dve.tensor_tensor(y[:, i, :], ps[:, Y0 + i, 0:D], b2_bc[:, bass.ds(e, 1), :].rearrange("p a d -> p (a d)"), ALU.add))
                        dve.tensor_scalar(y[:, i, :], y[:, i, :], y_w[:, i, bass.ds(e, 1)], None, ALU.mult).then_inc(s_y, 1)

                    rows_out(0)
                    rows_out(1)
                    chain.end()
                    dve.reg_add(g, g, 1)

            experts(dve, g, expert)

        @block.tensor
        def _(pe):
            for s in (s_kT, s_ctx, s_lg, s_f2):
                pe.sem_inc(s, TWO)
            pe.sem_inc(s_bt, ONE)

            pe.wait_ge(s_const, 1)
            pe.wait_ge(s_c, 32)
            pe.transpose(ps[:, 0, 0:C], c_rows[:, :], ident[0:C, 0:C])
            pe.transpose(ps[:, 0, 64:64 + E * M], b1_rows[:, :], ident[0:E * M, 0:E * M]).then_inc(s_cT, 1)
            pe.wait_ge(s_silu, 1)
            pe.wait_ge(s_wmod, 16)
            for n, k in enumerate((0, 1, 3, 4)):
                for c2 in range(C):
                    for c in range(C):
                        pe.matmul(ps[:, 1, n * C + c2:n * C + c2 + 1], wmod_sb[:, c, k * D + c2 * P:k * D + (c2 + 1) * P],
                                  silu_c[:, c:c + 1], start=c == 0, stop=c == C - 1)
            for n, k in enumerate((2, 5)):
                for c in range(C):
                    last = pe.matmul(ps[:, 2, n * D:(n + 1) * D], silu_b[:, c, :], wmod_sb[:, c, k * D:(k + 1) * D],
                                     start=c == 0, stop=c == C - 1)
            last.then_inc(s_mod, 1)

            def x_T(s, c, reuse):
                pe.wait_ge(s_xn, s + 1)
                if reuse:
                    pe.wait_ge(s_qs, s * ST - 1)
                for t in range(ST):
                    last = pe.transpose(ps[:, c, t * P:(t + 1) * P], xn[:, t, c * P:(c + 1) * P], ident[:, :])
                last.then_inc(s_xt, 1)

            def q_mm(s, i, reuse):
                if i == 0:
                    pe.wait_ge(s_hlo, s * C + C)
                if reuse:
                    pe.wait_ge(s_qs, s * ST + (i - 1))
                b = (i % 2) * 2
                tok = slice(i * P, (i + 1) * P)
                for half in range(2):
                    col = slice(half * 512, (half + 1) * 512)
                    for a, w, st, sp_ in three([((h_q[:, 0, c, tok], h_q[:, 1, c, tok]), (wqk_hi[:, c, col], wqk_lo[:, c, col])) for c in range(C)]):
                        last = pe.matmul(ps[:, b + half, :], a, w, start=st, stop=sp_)
                last.then_inc(s_q, 1)

            pe.wait_ge(s_cTc, 1)
            x_T(0, 0, False)
            pe.wait_ge(s_modr, 1)
            x_T(0, 1, False)
            pe.wait_ge(s_small, 48)
            for c in range(C):
                last = pe.matmul(ps[:, 3, 0:E], shift_b[:, c, :], wg_raw[:, c, :], start=c == 0, stop=c == C - 1)
            last.then_inc(s_bgp, 1)
            pe.wait_ge(s_fold_in, 32)
            for half in range(2):
                for j in range(4 * half, 4 * half + 4):
                    for c in range(C):
                        last = pe.transpose(ps[:, 4 + j // 2, (j % 2) * D + c * P:(j % 2) * D + (c + 1) * P],
                                            wv_raw[:, c, j * P:(j + 1) * P], ident[:, :])
                last.then_inc(s_wvT, 1)
            pe.wait_ge(s_wlqk, 2)
            pe.wait_ge(s_bgr, 1)
            for i in range(ST):
                q_mm(0, i, i >= 2)
            for c in range(C):
                x_T(1, c, True)
            q_mm(1, 0, True)
            pe.wait_ge(s_wvTc, 2)

            def body(s, more, more2):
                def k_mm(j):
                    if j == 0:
                        pe.wait_ge(s_hk, s * 16 + 16)
                    pe.wait_ge(s_ke, s * J + (j - 1 + TWO))
                    col = slice(HD + j * P, HD + (j + 1) * P)
                    hk = [[h_k[:, bass.ds(s & 1, 1), l, c, :].rearrange("p a t -> p (a t)") for l in range(2)] for c in range(C)]
                    for w, a, st, sp_ in three([((wqk_hi[:, c, col], wqk_lo[:, c, col]), hk[c]) for c in range(C)]):
                        last = pe.matmul(ps[:, KT + j % 2, :], w, a, start=st, stop=sp_)
                    last.then_inc(s_kt, 1)

                def k_T(j):
                    pe.wait_ge(s_ke, s * J + (j + 1 + TWO))
                    pe.wait_ge(s_klo, s * J + (j + TWO))
                    for t in range(ST):
                        last = pe.transpose(ps[:, TR, t * P:(t + 1) * P], k_exp[:, j % 2, t * P:(t + 1) * P], ident[:, :])
                    last.then_inc(s_kT, 1)

                def c_mm(j):
                    if j == 0:
                        pe.wait_ge(s_qlo, s * ST + ST)
                    pe.wait_ge(s_klo, s * J + (j + 1 + TWO))
                    pe.wait_ge(s_acc, s * J + (j + TWO))
                    for t in range(ST):
                        q = q_hl[:, bass.ds(s & 1, 1), t, j, :, :].rearrange("p a l d -> p (a l d)")
                        for n, kk in enumerate((k_hi, k_lo)):
                            last = pe.matmul(ps[:, CX, 0:2 * P], kk[:, j % 2, t, :], q, start=t == 0 and n == 0, stop=t == ST - 1 and n == 1)
                    last.then_inc(s_ctx, 1)

                for j in range(J):
                    k_mm(j)
                    if j >= 1:
                        k_T(j - 1)
                    if j >= 2:
                        c_mm(j - 2)
                    if more:
                        for slot, i in ((1, 1), (3, 2), (4, 3)):
                            if j == slot:
                                q_mm(s + 1, i, True)
                    if more2 and XT <= j < XT + C:
                        x_T(s + 2, j - XT, True)
                k_T(J - 1)
                c_mm(J - 2)
                if more2:
                    q_mm(s + 2, 0, True)
                c_mm(J - 1)

            superblocks(pe, body)

            pe.wait_ge(s_ctxn, 1)
            for j in range(J):
                last = pe.matmul(ps[:, j // 2, (j % 2) * D:(j % 2 + 1) * D], ctx_n[:, j, :], wout_sb[:, j, :], start=True, stop=True)
                if j % 2:
                    last.then_inc(s_cw, 1)
            for c in range(C):
                for j in range(J):
                    pe.wait_ge(s_cwc, j // 2 + 1)
                    last = pe.matmul(ps[:, 4 + c, 0:D], wvT[:, j, c * P:(c + 1) * P], cw[:, j, :], start=j == 0, stop=j == J - 1)
            last.then_inc(s_fold, 1)
            pe.wait_ge(s_foldr, 1)

            def attend(g, n):
                par, t = g % 2, g * GT + 2 * n
                if n == 0:
                    pe.wait_ge(s_hb[par], g // 2 * 64 + 64)
                pe.wait_ge(s_x1, t - 6 + EIGHT)
                for part in range(2):
                    pe.matmul(ps[:, AT + n % 4, :], ones_r[0:1, :], bo_hl[0:1, part, :, :].rearrange("p r d -> p (r d)"), start=part == 0, stop=False)
                for i in (2 * n, 2 * n + 1):
                    tok = slice((i % ST) * P, (i % ST + 1) * P)
                    h = h_b[:, par, :, i // ST, :, :]
                    o = ps[:, AT + n % 4, (i % 2) * D:(i % 2 + 1) * D]
                    for a, w, _, end in three([((h[:, 0, c, tok], h[:, 1, c, tok]), (fold_hi[:, c, :], fold_lo[:, c, :])) for c in range(C)]):
                        last = pe.matmul(o, a, w, start=False, stop=end and i % 2 == 1)
                last.then_inc(s_at, 2)

            def rows_T(g, n):
                t = g * GT + 2 * n
                pe.wait_ge(s_row, t + 2)
                pe.wait_ge(s_rTc, t // 2 - 1 + TWO)
                for i in range(2):
                    for c in range(C):
                        last = pe.transpose(ps[:, RT + n % 2, i * D + c * P:i * D + (c + 1) * P],
                                            rows[:, g % RB, 2 * n + i, c * P:(c + 1) * P], ident[:, :])
                last.then_inc(s_rT, 1)

            def logits(g, n):
                pe.wait_ge(s_rTc, g * GT // 2 + n + 1 + TWO)
                if n == 0:
                    pe.wait_ge(s_lgs, g + TWO)
                for i in range(2):
                    for c in range(C):
                        last = pe.matmul(ps[:, LG, (2 * n + i) * E:(2 * n + i + 1) * E],
                                         x1T[:, n % 2, i * D + c * P:i * D + (c + 1) * P], wg_mod[:, c, :],
                                         start=c == 0, stop=c == C - 1)
                last.then_inc(s_lg, 1)

            def ranks(g):
                par = g % 2
                pe.wait_ge(s_ch, g + 1)
                pe.wait_ge(s_spot, g + TWO)
                pe.matmul(ps[:, RK, 0:(GT + 1) * E], before_bf[:, :], chosen_bf[:, :, :], start=True, stop=False)
                for i in range(GT):
                    last = pe.matmul(ps[:, RK, (i + 1) * E:(GT + 1) * E], ones_bf[:, :],
                                     bc(chosen_bf[:, i, :], 1, [P, GT - i, E]), start=False, stop=i == GT - 1)
                last.then_inc(s_rk, 1)

            pairs = [divmod(q, GT // 2) for q in range(TILES // 2)]
            for q in range(AHEAD):
                attend(*pairs[q])
            rows_T(*pairs[0])
            for q in range(len(pairs)):
                new_group = q % (GT // 2) == GT // 2 - 1
                if not new_group:
                    rows_T(*pairs[q + 1])
                if q % (GT // 2) == 1 and q > 1:
                    ranks(pairs[q][0] - 1)
                if q + AHEAD < len(pairs):
                    attend(*pairs[q + AHEAD])
                logits(*pairs[q])
                if new_group and q + 1 < len(pairs):
                    rows_T(*pairs[q + 1])
            ranks(GROUPS - 1)

            pe.wait_ge(s_counts, 1)
            g = block_counter(pe, "g_pe")

            def block_T(n):
                pe.wait_ge(s_rows, n * 16 + 16)
                for c in range(C):
                    for i in range(BI):
                        last = pe.transpose(ps[:, XTB, c * BT + i * P:c * BT + (i + 1) * P], listed[:, i, c * P:(c + 1) * P], ident[:, :])
                last.then_inc(s_bt, 1)

            block_T(0)

            def expert(e, par, nb, last_expert):
                pe.wait_ge(s_wlo, e + 1)
                pe.sem_inc(s_turn_pe, 1)
                with pe.Fori(0, nb) as b:
                    gv = now(pe, g)
                    pe.wait_ge(s_blo, gv + 1)
                    for m in range(M):
                        k = m // 2
                        if m % 2 == 0:
                            pe.wait_ge(s_gelu, gv * 4 + (k + 1))
                        col = slice(m * P, (m + 1) * P)
                        for w, a, st, sp_ in three([((w1_hi[par][:, c, col], w1_lo[par][:, c, col]), (xT_hi[:, c, :], xT_lo[:, c, :])) for c in range(C)]):
                            last = pe.matmul(ps[:, k, (m % 2) * BT:(m % 2 + 1) * BT], w, a, start=st, stop=sp_)
                        if m % 2:
                            last.then_inc(s_f1, 1)

                    def second(i, chunks):
                        if 0 in chunks:
                            pe.wait_ge(s_y, gv * 2 + (i + 1))
                        r = slice(i * P, (i + 1) * P)
                        for m in chunks:
                            if i == 0 and m % 2 == 0:
                                pe.wait_ge(s_hid, gv * 4 + (m // 2 + 1 + FOUR))
                            for a, w, st, sp_ in three([((hid_hi[:, m, r], hid_lo[:, m, r]), (w2_hi[par][:, m, :], w2_lo[par][:, m, :]))]):
                                last = pe.matmul(ps[:, Y0 + i, 0:D], a, w, start=m == 0 and st, stop=m == M - 1 and sp_)
                        if M - 1 in chunks:
                            last.then_inc(s_f2, 1)

                    second(0, range(0, M - 2))
                    block_T(gv + 1)
                    second(1, range(0, M - 2))
                    second(0, range(M - 2, M))
                    second(1, range(M - 2, M))
                    pe.reg_add(g, g, 1)

            experts(pe, g, expert)


_INS = ['L0_attn_x', 'L0_attn_w_qkv', 'L0_attn_w_out', 'L0_attn_b_out', 'L0_ffn_Wg', 'L0_ffn_bg', 'L0_ffn_W1',
        'L0_ffn_b1', 'L0_ffn_W2', 'L0_ffn_b2', 'L0_c', 'L0_wmod']


def kernel(**inputs):
    import numpy as _np
    import concourse.bacc as _bacc
    from concourse import mybir as _mybir
    from concourse.bass_utils import run_bass_kernel_spmd as _run

    nc = _bacc.Bacc("TRN2", target_bir_lowering=False, num_devices=1)
    arrays, args = {}, []
    for name in _INS:
        a = _np.ascontiguousarray(inputs[name])
        arrays[f"in_{name}"] = a
        args.append(nc.dram_tensor(f"in_{name}", a.shape, _mybir.dt.from_np(a.dtype), kind="ExternalInput").ap())
    args.append(nc.dram_tensor("out", (N + BT, D), _mybir.dt.float32, kind="ExternalOutput").ap())
    adaln_block(nc, *args)
    r = _run(nc, [arrays], core_ids=[0])
    return r.results[0]["out"][:N].reshape(1, N, D)
```
